# Optimizing a Trainium2 kernel written in Bass

```python
import numpy as np
import jax
import jax.numpy as jnp

def _softmax(x, axis=-1):
    return jax.nn.softmax(x, axis=axis)

def _gelu(x):
    return jax.nn.gelu(x, approximate=True)

def _silu(x):
    return jax.nn.silu(x)

def _sigmoid(x):
    return jax.nn.sigmoid(x)

def _layernorm(x, axis=-1, eps=1e-05):
    m = jnp.mean(x, axis=axis, keepdims=True)
    v = jnp.var(x, axis=axis, keepdims=True)
    return (x - m) / jnp.sqrt(v + eps)

def _scatter_add(tgt, idx, src, axis=0):
    return tgt.at[idx].add(src)

def _segment_sum(src, seg, n):
    return jax.ops.segment_sum(src, seg, n)
kernel_name = 'mk_decoder_preln_d1_seqx_r8_a9c4f9'

def setup_inputs(seed: int=0):
    np.random.seed(seed)
    _w = jnp.asarray

    def _rec_inputs():
        import jax
        import jax.numpy as jnp
        _rk = jax.random.key(seed)
        x = -0.0002928 + 1 * jax.random.normal(jax.random.fold_in(_rk, 1), (32, 100, 256), jnp.float32)
        _lenS = 100 - jax.random.randint(jax.random.fold_in(_rk, 7), (32,), 0, max(1, 100 // 4) + 1, jnp.int32)
        _lenS2 = 1444 - jax.random.randint(jax.random.fold_in(_rk, 8), (32,), 0, max(1, 1444 // 4) + 1, jnp.int32)
        _ctx_512P = jax.random.normal(jax.random.fold_in(_rk, 11), (32, 16, 64), jnp.float32)
        _ctx_512c = jax.random.dirichlet(jax.random.fold_in(_rk, 511), 0.3 * jnp.ones((16,), jnp.float32), (32, 1444))
        _ctx_512t = jnp.einsum('bsk,bkd->bsd', _ctx_512c, _ctx_512P)
        _ctx_512t = _ctx_512t * jax.lax.rsqrt(jnp.mean(jnp.square(_ctx_512t)) + 1e-12) * 0.953939
        ctx_512 = 0.000227908 + 0.99994 * (_ctx_512t + 0.3 * jax.random.normal(jax.random.fold_in(_rk, 611), (32, 1444, 64), jnp.float32))
        return (x, ctx_512)
    x, ctx_512 = _rec_inputs()

    def _L0_attn_setup():
        import jax, jax.numpy as jnp
        import numpy as np
        B, S, E, H = (2, 256, 256, 16)
        HD = E // H
        EPS = 1e-05

        def _retention(x, Wq, bq, Wk, bk, Wv, bv, Wg, bg, Wo, bo, gn_w, gn_b, decay):
            b, s, e = x.shape
            h = decay.shape[0]
            hd = e // h
            scaling = hd ** (-0.5)

            def heads(t):
                return t.reshape(b, s, h, hd).transpose(0, 2, 1, 3)
            q = heads((x @ Wq + bq) * scaling)
            k = heads(x @ Wk + bk)
            v = heads(x @ Wv + bv)
            idx = jnp.arange(s)
            diff = idx[:, None] - idx[None, :]
            causal = diff >= 0
            diff_c = jnp.where(causal, diff, 0).astype(jnp.float32)
            D = jnp.where(causal[None], jnp.exp(decay[:, None, None] * diff_c[None]), 0.0)
            ret = jnp.einsum('bhid,bhjd->bhij', q, k) * D[None]
            scale = jnp.clip(jnp.abs(jax.lax.stop_gradient(ret).sum(-1, keepdims=True)), 1.0, None)
            ret = ret / scale
            attn = jnp.einsum('bhij,bhjd->bhid', ret, v)
            attn = attn.transpose(0, 2, 1, 3).reshape(b, s, e)
            g = attn.reshape(b, s, h, hd)
            mu = g.mean(-1, keepdims=True)
            var = g.var(-1, keepdims=True)
            g = (g - mu) / jnp.sqrt(var + EPS)
            g = g.reshape(b, s, e) * gn_w + gn_b
            gate = jax.nn.silu(x @ Wg + bg)
            return gate * g @ Wo + bo
        key = jax.random.key(seed)
        ks = jax.random.split(key, 12)
        std = 0.02

        def lin(k, din, dout):
            kw, kb = jax.random.split(k)
            W = jax.random.normal(kw, (din, dout), jnp.float32) * std
            b = jnp.zeros((dout,), jnp.float32)
            return (W, b)
        x = jax.random.normal(ks[0], (B, S, E), jnp.float32)
        Wq, bq = lin(ks[1], E, E)
        Wk, bk = lin(ks[2], E, E)
        Wv, bv = lin(ks[3], E, E)
        Wg, bg = lin(ks[4], E, E)
        Wo, bo = lin(ks[5], E, E)
        gn_w = jnp.ones((E,), jnp.float32)
        gn_b = jnp.zeros((E,), jnp.float32)
        decay = jnp.log(1.0 - 2.0 ** (-5.0 - jnp.arange(H, dtype=jnp.float32)))
        return dict(x=x, Wq=Wq, bq=bq, Wk=Wk, bk=bk, Wv=Wv, bv=bv, Wg=Wg, bg=bg, Wo=Wo, bo=bo, gn_w=gn_w, gn_b=gn_b, decay=decay)
    _L0_attn_all = _L0_attn_setup()
    _L0_attn_in = {k: v for k, v in _L0_attn_all.items() if k in ('Wq', 'bq', 'Wk', 'bk', 'Wv', 'bv', 'Wg', 'bg', 'Wo', 'bo', 'gn_w', 'gn_b', 'decay')}
    del _L0_attn_all

    def _L0_xattn_setup():
        import jax, jax.numpy as jnp
        import numpy as np
        B, S, L = (2, 128, 128)
        DIM_Q, H, K, D_C, D_CQ, R = (256, 16, 128, 64, 192, 64)

        def _rope_tables(length, dim):
            inv = 1.0 / 10000.0 ** (jnp.arange(0, dim, 2, dtype=jnp.float32) / dim)
            f = jnp.arange(length, dtype=jnp.float32)[:, None] * inv[None, :]
            sin = jnp.repeat(jnp.sin(f), 2, axis=-1)
            cos = jnp.repeat(jnp.cos(f), 2, axis=-1)
            return (sin, cos)

        def _rotate_half(x):
            half = x.shape[-1] // 2
            return jnp.concatenate([-x[..., half:], x[..., :half]], axis=-1)

        def _apply_rope(x, sin, cos):
            return x * cos + _rotate_half(x) * sin
        key = jax.random.key(seed)
        ks = jax.random.split(key, 8)
        return {'hidden_q': jax.random.normal(ks[0], (B, S, DIM_Q), jnp.float32), 'kv_c': jax.random.normal(ks[1], (B, L, D_C), jnp.float32), 'Wq': jax.random.normal(ks[2], (H * K, DIM_Q), jnp.float32) / np.sqrt(DIM_Q).astype(np.float32), 'w_kc_q': jax.random.normal(ks[3], (H, K, D_CQ), jnp.float32) / np.sqrt(K).astype(np.float32), 'w_kc_kv': jax.random.normal(ks[4], (H, K, D_C), jnp.float32) / np.sqrt(K).astype(np.float32), 'W_qr': jax.random.normal(ks[5], (H, D_CQ, R), jnp.float32) / np.float32(np.sqrt(D_CQ) * np.sqrt(R)), 'W_kr': jax.random.normal(ks[6], (H, D_C, R), jnp.float32) / np.sqrt(D_C).astype(np.float32), 'Wo': jax.random.normal(ks[7], (DIM_Q, H * K), jnp.float32) / np.sqrt(H * K).astype(np.float32)}
    _L0_xattn_all = _L0_xattn_setup()
    _L0_xattn_in = {k: v for k, v in _L0_xattn_all.items() if k in ('Wq', 'w_kc_q', 'w_kc_kv', 'W_qr', 'W_kr', 'Wo')}
    del _L0_xattn_all

    def _L0_ffn_setup():
        import jax, jax.numpy as jnp
        import numpy as np
        EPS = 1e-08

        def _quantize(w):
            gamma = jnp.mean(jnp.abs(w))
            return jnp.clip(jnp.round(w / (gamma + EPS)), -1.0, 1.0)

        def _bitlinear(x, w):
            return jnp.matmul(x, _quantize(w).T)
        key = jax.random.key(seed)
        k1, k2, k3, k4 = jax.random.split(key, 4)
        d, h = (256, 704)
        x = jax.random.normal(k1, (4, 256, d), dtype=jnp.float32)
        w1 = jax.random.normal(k2, (h, d), dtype=jnp.float32)
        w2 = jax.random.normal(k3, (h, d), dtype=jnp.float32)
        w3 = jax.random.normal(k4, (d, h), dtype=jnp.float32)
        return {'x': x, 'w1': w1, 'w2': w2, 'w3': w3}
    _L0_ffn_all = _L0_ffn_setup()
    _L0_ffn_in = {k: v for k, v in _L0_ffn_all.items() if k in ('w1', 'w2', 'w3')}
    del _L0_ffn_all
    return {'x': x, 'ctx_512': ctx_512, 'L0_attn_Wq': _L0_attn_in['Wq'], 'L0_attn_bq': _L0_attn_in['bq'], 'L0_attn_Wk': _L0_attn_in['Wk'], 'L0_attn_bk': _L0_attn_in['bk'], 'L0_attn_Wv': _L0_attn_in['Wv'], 'L0_attn_bv': _L0_attn_in['bv'], 'L0_attn_Wg': _L0_attn_in['Wg'], 'L0_attn_bg': _L0_attn_in['bg'], 'L0_attn_Wo': _L0_attn_in['Wo'], 'L0_attn_bo': _L0_attn_in['bo'], 'L0_attn_gn_w': _L0_attn_in['gn_w'], 'L0_attn_gn_b': _L0_attn_in['gn_b'], 'L0_attn_decay': _L0_attn_in['decay'], 'L0_xattn_Wq': _L0_xattn_in['Wq'], 'L0_xattn_w_kc_q': _L0_xattn_in['w_kc_q'], 'L0_xattn_w_kc_kv': _L0_xattn_in['w_kc_kv'], 'L0_xattn_W_qr': _L0_xattn_in['W_qr'], 'L0_xattn_W_kr': _L0_xattn_in['W_kr'], 'L0_xattn_Wo': _L0_xattn_in['Wo'], 'L0_ffn_w1': _L0_ffn_in['w1'], 'L0_ffn_w2': _L0_ffn_in['w2'], 'L0_ffn_w3': _L0_ffn_in['w3']}

def reference(x, ctx_512, L0_attn_Wq, L0_attn_bq, L0_attn_Wk, L0_attn_bk, L0_attn_Wv, L0_attn_bv, L0_attn_Wg, L0_attn_bg, L0_attn_Wo, L0_attn_bo, L0_attn_gn_w, L0_attn_gn_b, L0_attn_decay, L0_xattn_Wq, L0_xattn_w_kc_q, L0_xattn_w_kc_kv, L0_xattn_W_qr, L0_xattn_W_kr, L0_xattn_Wo, L0_ffn_w1, L0_ffn_w2, L0_ffn_w3):
    import jax
    import jax.numpy as jnp

    def _L0_attn_ref(x, Wq, bq, Wk, bk, Wv, bv, Wg, bg, Wo, bo, gn_w, gn_b, decay):
        import jax, jax.numpy as jnp
        import numpy as np
        B, S, E, H = (2, 256, 256, 16)
        HD = E // H
        EPS = 1e-05

        def _retention(x, Wq, bq, Wk, bk, Wv, bv, Wg, bg, Wo, bo, gn_w, gn_b, decay):
            b, s, e = x.shape
            h = decay.shape[0]
            hd = e // h
            scaling = hd ** (-0.5)

            def heads(t):
                return t.reshape(b, s, h, hd).transpose(0, 2, 1, 3)
            q = heads((x @ Wq + bq) * scaling)
            k = heads(x @ Wk + bk)
            v = heads(x @ Wv + bv)
            idx = jnp.arange(s)
            diff = idx[:, None] - idx[None, :]
            causal = diff >= 0
            diff_c = jnp.where(causal, diff, 0).astype(jnp.float32)
            D = jnp.where(causal[None], jnp.exp(decay[:, None, None] * diff_c[None]), 0.0)
            ret = jnp.einsum('bhid,bhjd->bhij', q, k) * D[None]
            scale = jnp.clip(jnp.abs(jax.lax.stop_gradient(ret).sum(-1, keepdims=True)), 1.0, None)
            ret = ret / scale
            attn = jnp.einsum('bhij,bhjd->bhid', ret, v)
            attn = attn.transpose(0, 2, 1, 3).reshape(b, s, e)
            g = attn.reshape(b, s, h, hd)
            mu = g.mean(-1, keepdims=True)
            var = g.var(-1, keepdims=True)
            g = (g - mu) / jnp.sqrt(var + EPS)
            g = g.reshape(b, s, e) * gn_w + gn_b
            gate = jax.nn.silu(x @ Wg + bg)
            return gate * g @ Wo + bo
        return _retention(x, Wq, bq, Wk, bk, Wv, bv, Wg, bg, Wo, bo, gn_w, gn_b, decay)

    def _L0_xattn_ref(hidden_q, kv_c, Wq, w_kc_q, w_kc_kv, W_qr, W_kr, Wo):
        import jax, jax.numpy as jnp
        import numpy as np
        B, S, L = (2, 128, 128)
        DIM_Q, H, K, D_C, D_CQ, R = (256, 16, 128, 64, 192, 64)

        def _rope_tables(length, dim):
            inv = 1.0 / 10000.0 ** (jnp.arange(0, dim, 2, dtype=jnp.float32) / dim)
            f = jnp.arange(length, dtype=jnp.float32)[:, None] * inv[None, :]
            sin = jnp.repeat(jnp.sin(f), 2, axis=-1)
            cos = jnp.repeat(jnp.cos(f), 2, axis=-1)
            return (sin, cos)

        def _rotate_half(x):
            half = x.shape[-1] // 2
            return jnp.concatenate([-x[..., half:], x[..., :half]], axis=-1)

        def _apply_rope(x, sin, cos):
            return x * cos + _rotate_half(x) * sin
        Bv, Sv, _ = hidden_q.shape
        _, Lv, _ = kv_c.shape
        q_hk = (hidden_q @ Wq.T).reshape(Bv, Sv, H, K)
        q_big = jnp.einsum('bshk,hkq->bshq', q_hk, w_kc_q)
        sin_q, cos_q = _rope_tables(Sv, D_CQ)
        q_big = _apply_rope(q_big, sin_q[None, :, None, :], cos_q[None, :, None, :])
        sin_k, cos_k = _rope_tables(Lv, D_C)
        kv_r = _apply_rope(kv_c, sin_k[None], cos_k[None])
        q_r = jnp.einsum('bshq,hqr->bhsr', q_big, W_qr)
        k_r = jnp.einsum('bld,hdr->bhlr', kv_r, W_kr)
        scores = jnp.einsum('bhsr,bhlr->bhsl', q_r, k_r)
        attn = jax.nn.softmax(scores, axis=-1)
        ctx_c = jnp.einsum('bhsl,bld->bhsd', attn, kv_r)
        ctx_lat = jnp.einsum('bhsd,hkd->bhsk', ctx_c, w_kc_kv)
        ctx = ctx_lat.transpose(0, 2, 1, 3).reshape(Bv, Sv, H * K)
        return ctx @ Wo.T

    def _L0_ffn_ref(x, w1, w2, w3):
        import jax, jax.numpy as jnp
        import numpy as np
        EPS = 1e-08

        def _quantize(w):
            gamma = jnp.mean(jnp.abs(w))
            return jnp.clip(jnp.round(w / (gamma + EPS)), -1.0, 1.0)

        def _bitlinear(x, w):
            return jnp.matmul(x, _quantize(w).T)
        x1 = _bitlinear(x, w1)
        x2 = _bitlinear(x, w2)
        hidden = jax.nn.sigmoid(x1) * x2
        return _bitlinear(hidden, w3)
    x = x + _L0_attn_ref(_layernorm(x, axis=-1), L0_attn_Wq, L0_attn_bq, L0_attn_Wk, L0_attn_bk, L0_attn_Wv, L0_attn_bv, L0_attn_Wg, L0_attn_bg, L0_attn_Wo, L0_attn_bo, L0_attn_gn_w, L0_attn_gn_b, L0_attn_decay)
    x = x + _L0_xattn_ref(_layernorm(x, axis=-1), ctx_512, L0_xattn_Wq, L0_xattn_w_kc_q, L0_xattn_w_kc_kv, L0_xattn_W_qr, L0_xattn_W_kr, L0_xattn_Wo)
    x = x + _L0_ffn_ref(_layernorm(x, axis=-1), L0_ffn_w1, L0_ffn_w2, L0_ffn_w3)
    return x

_drawn_inputs = setup_inputs


def setup_inputs(seed=0):
    import zlib

    import numpy as np

    out = dict(_drawn_inputs(seed))
    spreads = {'L0_attn_bq': (0.0, 0.1),
     'L0_attn_bk': (0.0, 0.1),
     'L0_attn_bv': (0.0, 0.1),
     'L0_attn_bg': (0.0, 0.274),
     'L0_attn_bo': (0.0, 0.1),
     'L0_attn_gn_w': (1.0, 0.6),
     'L0_attn_gn_b': (0.0, 0.8)}
    factors = {'L0_attn_decay': 5.676}
    for name, (base, spread) in spreads.items():
        noise = np.random.default_rng([zlib.crc32(name.encode()), seed]).standard_normal(out[name].shape)
        drawn = base * np.exp(spread * noise) if base else spread * noise
        out[name] = jnp.asarray(drawn.astype(out[name].dtype))
    for name, factor in factors.items():
        out[name] = (out[name] * factor).astype(out[name].dtype)
    return out
```

```python
from contextlib import ExitStack

import numpy as np

import concourse.bass as bass
from concourse import mybir

F32 = mybir.dt.float32
F32R = mybir.dt.float32r
ALU = mybir.AluOpType
ACT = mybir.ActivationFunctionType
AX = mybir.AxisListType

B, S, E = 32, 100, 256
H, HD = 16, 16
L, DC = 1444, 64
K, DQ, R = 128, 192, 64
F = 704
P = 128
EC = E // P
GB = 4
NG = B // GB
GT = GB * S
EPS = 1e-5


class Signal:

    def __init__(self, ctx, nc, name, each, credit=0):
        self.sem = ctx.enter_context(nc.semaphore(name))
        self.each, self.credit = each, credit

    def at(self, k, count):
        return k * self.each + (count + self.credit)


class Transfer:

    def __init__(self, ctx, nc, name, credit=0, amount=16):
        self.sems = [ctx.enter_context(nc.semaphore(name + str(parity))) for parity in range(2)]
        self.credit, self.amount = credit, amount

    def done(self, k, parity):
        return k * (self.amount // 2) + (self.amount - self.amount // 2 * parity + self.credit)


def for_groups(eng, slot):
    with eng.Fori(0, (NG - 2) // 2) as i:
        for parity in range(2):
            slot(i * 2 + parity, parity, True)
    slot(NG - 2, 0, True)
    slot(NG - 1, 1, False)


def phase_retention(nc, d):
    with ExitStack() as ctx:
        def sb(name, shape, dt=F32):
            return ctx.enter_context(nc.sbuf_tensor("a_" + name, shape, dt))

        def ps(name, shape):
            return ctx.enter_context(nc.psum_tensor("a_" + name, shape, F32))

        def sig(name, each, credit=0):
            return Signal(ctx, nc, "a_" + name, each, credit)

        wqk = sb("wqk", [P, 2, EC, E])
        wvg = sb("wvg", [P, EC, 2 * E])
        wo = sb("wo", [P, EC, E])
        bqk = sb("bqk", [P, 2, EC])
        bvg = sb("bvg", [S, 2 * E])
        gnw = sb("gnw", [S, E])
        gnb = sb("gnb", [S, E])
        bo = sb("bo", [S, E])
        decay = sb("decay", [S, H])
        rel = sb("rel", [S, S])
        causal = sb("causal", [S, S])
        headmask = sb("headmask", [P, 8])
        ident = sb("ident", [P, P])
        dmask = sb("dmask", [S, H, S])
        mhalf = sb("mhalf", [S, GB * H])
        x = sb("x", [S, 2, GB, E])
        stats = sb("stats", [S, GB, 6])
        mv = sb("mv", [S, GB, 2])
        veps = sb("veps", [S, GB])
        rstd = sb("rstd", [S, GB])
        xn = sb("xn", [S, GB, E])
        xnT = sb("xnT", [P, EC, GT])
        qkT = sb("qkT", [P, 2, 2, EC, GT])
        vaug = sb("vaug", [S, 2, GB, H, 2 * HD])
        z = sb("z", [S, 2, GB, E])
        qm = sb("qm", [P, 2, EC, 8, S])
        ret = sb("ret", [S, 2, H, S])
        av = sb("av", [P, GT])
        neg = sb("neg", [S, GB, H])
        den = sb("den", [S, GB, H])
        rec = sb("rec", [S, GB, H])
        att = sb("att", [S, GB * H, HD])
        s1 = sb("s1", [S, GB * H])
        mean = sb("mean", [S, GB * H])
        cent = sb("cent", [S, GB * H, HD])
        sq = sb("sq", [S, GB * H, HD])
        s2 = sb("s2", [S, GB * H])
        gveps = sb("gveps", [S, GB * H])
        grstd = sb("grstd", [S, GB * H])
        gn = sb("gn", [S, GB, E])
        th = sb("th", [S, GB, E])
        gate = sb("gate", [S, GB, E])
        y = sb("y", [S, GB, E])
        yT = sb("yT", [P, EC, GT])
        xb = sb("xb", [S, GB, E])
        x1 = sb("x1", [S, 2, GB, E])

        ring = ps("ring", [P, 2, 512])
        sc = ps("sc", [P, 4, 512])
        pav = ps("pav", [P, 512])
        pt = ps("pt", [P, 512])

        weights_loaded = sig("weights_loaded", 0)
        decay_exp = sig("decay_exponentials", 0)
        mask_ready = sig("decay_mask_ready", 0)
        constants = sig("constants_set", 0)
        gn_halved = sig("gn_halved", 0)
        x_loaded = Transfer(ctx, nc, "a_x_loaded")
        row_stats = sig("row_stats", GB)
        stats_complete = sig("row_stats_complete", 1)
        row_mv = sig("row_mean_var", GB)
        row_veps = sig("row_var_eps", 1)
        row_rstd = sig("row_rstd", 1)
        xn_ready = sig("xn_ready", GB, GB)
        unit = sig("ring_unit_filled", 10, 10)
        act_read = sig("ring_unit_read_by_act", 6, 6)
        dve_read = sig("ring_unit_read_by_dve", 8, 8)
        q_spread = sig("q_spread", 8, 16)
        sc_filled = sig("scores_filled", 16, 32)
        sc_masked = sig("scores_masked", 16, 16)
        av_filled = sig("attn_filled", GB, 8)
        av_copied = sig("attn_copied", GB)
        av_turned = sig("attn_turned", GB)
        sums_negated = sig("row_sums_negated", GB)
        sums_clipped = sig("row_sums_clipped", GB)
        sums_inverted = sig("row_sums_inverted", GB)
        att_scaled = sig("attn_scaled", GB)
        gn_sum = sig("gn_sum", 1)
        gn_mean = sig("gn_mean", 1)
        gn_centred = sig("gn_centred", 1)
        gn_squared = sig("gn_squared", 1)
        gn_sqsum = sig("gn_square_sum", 1)
        gn_veps = sig("gn_var_eps", 1)
        gn_rstd = sig("gn_rstd", 1)
        gn_scaled = sig("gn_scaled", 1)
        gn_weighted = sig("gn_weighted", 1)
        gn_shifted = sig("gn_shifted", 1)
        gate_tanh = sig("gate_tanh", 1)
        gate_ready = sig("gate_ready", 1)
        y_ready = sig("y_ready", 1)
        y_turned = sig("y_turned", EC)
        yT_copied = sig("yT_copied", EC)
        o_filled = sig("o_filled", GB)
        res_biased = sig("residual_biased", 1)
        x1_ready = sig("x1_ready", GB, 2 * GB)
        x1_stored = Transfer(ctx, nc, "a_x1_stored", 16)

        weights = (
            (wqk[:, 0], d["Wq"].rearrange("(c p) n -> p c n", p=P)),
            (wqk[:, 1], d["Wk"].rearrange("(c p) n -> p c n", p=P)),
            (wvg[:, :, 0:E], d["Wv"].rearrange("(c p) n -> p c n", p=P)),
            (wvg[:, :, E:2 * E], d["Wg"].rearrange("(c p) n -> p c n", p=P)),
            (wo[:], d["Wo"].rearrange("(c p) n -> p c n", p=P)),
            (bqk[:, 0], d["bq"]), (bqk[:, 1], d["bk"]),
            (bvg[:, 0:E], d["bv"]), (bvg[:, E:2 * E], d["bg"]), (gnw[:], d["gn_w"]), (gnb[:], d["gn_b"]),
            (bo[:], d["bo"]), (decay[:], d["decay"]), (rel[:], d["rel"]), (causal[:], d["causal"]),
            (headmask[:], d["headmask"]), (ident[:], d["ident"]),
        )
        W_ALL = 16 * len(weights)
        block = ctx.enter_context(nc.Block())

        @block.sync
        def _(sp):
            def load(k, parity):
                sp.wait_ge(x1_ready.sem, x1_ready.at(k - 2, GB))
                src = d["x"][bass.ds(k * GB, GB)].rearrange("b s e -> s b e")
                sp.dma_start(x[:, parity], src).then_inc(x_loaded.sems[parity], 16)

            def store(k, parity):
                sp.wait_ge(x1_ready.sem, x1_ready.at(k, GB))
                dst = d["x1"][bass.ds(k * GB, GB)].rearrange("b s e -> s b e")
                sp.dma_start(dst, x1[:, parity]).then_inc(x1_stored.sems[parity], 16)

            def slot(k, parity, more):
                if more:
                    load(k + 1, 1 - parity)
                store(k, parity)

            for parity in range(2):
                sp.sem_inc(x1_stored.sems[parity], x1_stored.credit)
            load(0, 0)
            for dst, src in weights:
                sp.dma_start(dst, src).then_inc(weights_loaded.sem, 16)
            for_groups(sp, slot)
            for parity in range(2):
                sp.wait_ge(x1_stored.sems[parity], x1_stored.done(NG - 2 + parity, parity))

        @block.gpsimd
        def _(pool):
            pool.memset(mhalf[:], -0.5).then_inc(constants.sem, 1)
            pool.memset(vaug[:], 1.0).then_inc(constants.sem, 1)
            pool.wait_ge(weights_loaded.sem, W_ALL)
            pool.tensor_scalar(gnw[:], gnw[:], 0.5, 1.0, ALU.mult, ALU.mult).then_inc(gn_halved.sem, 1)
            pool.tensor_scalar(gnb[:], gnb[:], 0.5, 1.0, ALU.mult, ALU.mult).then_inc(gn_halved.sem, 1)
            pool.sem_inc(q_spread.sem, q_spread.credit)
            pool.wait_ge(constants.sem, 2)
            pool.wait_ge(gn_halved.sem, 2)

            def rows_rstd(k):
                pool.wait_ge(row_veps.sem, row_veps.at(k, 1))
                pool.tensor_tensor(rstd[:], veps[:], mhalf[:, 0:GB], ALU.pow).then_inc(row_rstd.sem, 1)

            def spread(k, parity, b):
                pool.wait_ge(sc_filled.sem, sc_filled.at(k, 4 * b - 4))
                for c in range(EC):
                    pool.tensor_tensor(
                        qm[:, b % 2, c],
                        qkT[:, parity, 0, c, b * S:(b + 1) * S].unsqueeze(1).broadcast_to([P, 8, S]),
                        headmask[:].unsqueeze(2).broadcast_to([P, 8, S]),
                        ALU.mult).then_inc(q_spread.sem, 1)

            def slot(k, parity, more):
                pool.wait_ge(x_loaded.sems[parity], x_loaded.done(k, parity))
                pool.wait_ge(x1_ready.sem, x1_ready.at(k, 0))
                pool.tensor_tensor(xb[:], x[:, parity], bo[:].unsqueeze(1).broadcast_to([S, GB, E]),
                                   ALU.add).then_inc(res_biased.sem, 1)
                pool.wait_ge(act_read.sem, act_read.at(k, 4))
                spread(k, parity, 0)
                if more:
                    rows_rstd(k + 1)
                for b in range(1, GB):
                    spread(k, parity, b)
                pool.wait_ge(gn_veps.sem, gn_veps.at(k, 1))
                pool.tensor_tensor(grstd[:], gveps[:], mhalf[:], ALU.pow).then_inc(gn_rstd.sem, 1)
                pool.wait_ge(gn_scaled.sem, gn_scaled.at(k, 1))
                pool.tensor_tensor(gn[:], gn[:], gnw[:].unsqueeze(1).broadcast_to([S, GB, E]),
                                   ALU.mult).then_inc(gn_weighted.sem, 1)
                pool.wait_ge(gn_weighted.sem, gn_weighted.at(k, 1))
                pool.tensor_tensor(gn[:], gn[:], gnb[:].unsqueeze(1).broadcast_to([S, GB, E]),
                                   ALU.add).then_inc(gn_shifted.sem, 1)

            rows_rstd(0)
            for_groups(pool, slot)

        @block.scalar
        def _(act):
            act.wait_ge(weights_loaded.sem, W_ALL)
            act.sem_inc(act_read.sem, act_read.credit)
            for h in range(H):
                act.activation(dmask[:, h], rel[:], ACT.Exp, scale=decay[:, h:h + 1]).then_inc(decay_exp.sem, 1)

            def copy_xnT(k):
                act.wait_ge(unit.sem, unit.at(k - 1, 10))
                for c in range(EC):
                    act.wait_ge(unit.sem, unit.at(k, c + 1))
                    act.copy(xnT[:, c], ring[:, c, 0:GT]).then_inc(act_read.sem, 1)

            def copy_qk(k, parity):
                act.wait_ge(q_spread.sem, q_spread.at(k - 2, 8))
                act.wait_ge(sc_filled.sem, sc_filled.at(k - 2, 16))
                for w in range(2):
                    for c in range(EC):
                        u = 2 + 2 * w + c
                        act.wait_ge(unit.sem, unit.at(k, u + 1))
                        act.activation(qkT[:, parity, w, c], ring[:, u % 2, 0:GT], ACT.Identity,
                                       bias=bqk[:, w, c:c + 1]).then_inc(act_read.sem, 1)

            def slot(k, parity, more):
                act.wait_ge(dve_read.sem, dve_read.at(k, 8))
                act.wait_ge(gate_ready.sem, gate_ready.at(k, 0))
                act.activation(th[:], z[:, parity], ACT.Tanh, scale=0.5).then_inc(gate_tanh.sem, 1)
                for b in range(GB):
                    if b == 1 and more:
                        copy_xnT(k + 1)
                    act.wait_ge(av_filled.sem, av_filled.at(k, b + 1))
                    act.wait_ge(av_turned.sem, av_turned.at(k, b))
                    act.copy(av[:], pav[:, 0:GT]).then_inc(av_copied.sem, 1)
                if more:
                    copy_qk(k + 1, 1 - parity)
                act.wait_ge(gn_centred.sem, gn_centred.at(k, 1))
                act.activation(sq[:], cent[:], ACT.Square).then_inc(gn_squared.sem, 1)
                act.wait_ge(o_filled.sem, o_filled.at(k, 0))
                for c, bank in enumerate((pav, pt)):
                    act.wait_ge(y_turned.sem, y_turned.at(k, c + 1))
                    act.copy(yT[:, c], bank[:, 0:GT]).then_inc(yT_copied.sem, 1)

            copy_xnT(0)
            copy_qk(0, 0)
            for_groups(act, slot)

        @block.vector
        def _(dve):
            dve.sem_inc(xn_ready.sem, xn_ready.credit)
            dve.sem_inc(dve_read.sem, dve_read.credit)
            dve.sem_inc(sc_masked.sem, sc_masked.credit)
            dve.sem_inc(x1_ready.sem, x1_ready.credit)

            def row_statistics(k, parity):
                dve.wait_ge(x_loaded.sems[parity], x_loaded.done(k, parity))
                for b in range(GB):
                    dve.bn_stats(stats[:, b], x[:, parity, b]).then_inc(row_stats.sem, 1)
                dve.wait_ge(row_stats.sem, row_stats.at(k, GB))
                dve.sem_inc(stats_complete.sem, 1)
                for b in range(GB):
                    dve.bn_aggr(mv[:, b], stats[:, b]).then_inc(row_mv.sem, 1)
                dve.wait_ge(row_mv.sem, row_mv.at(k, GB))
                dve.tensor_scalar(veps[:], mv[:, :, 1], EPS, None, ALU.add).then_inc(row_veps.sem, 1)

            def normalise(k, parity):
                dve.wait_ge(row_rstd.sem, row_rstd.at(k, 1))
                dve.wait_ge(unit.sem, unit.at(k - 1, 2))
                for b in range(GB):
                    dve.tensor_scalar(xn[:, b], x[:, parity, b], mv[:, b, 0:1], rstd[:, b:b + 1],
                                      ALU.subtract, ALU.mult).then_inc(xn_ready.sem, 1)

            def read_vg(k, parity, b):
                u = 6 + b
                dve.wait_ge(unit.sem, unit.at(k, u + 1))
                dve.tensor_tensor(vaug[:, parity, b, :, 0:HD],
                                  ring[0:S, u % 2, 0:E].rearrange("p (h e) -> p h e", h=H),
                                  bvg[:, 0:E].rearrange("p (h e) -> p h e", h=H),
                                  ALU.add).then_inc(dve_read.sem, 1)
                dve.tensor_tensor(z[:, parity, b], ring[0:S, u % 2, E:2 * E], bvg[:, E:2 * E],
                                  ALU.add).then_inc(dve_read.sem, 1)

            def mask_scores(k, b):
                dve.wait_ge(av_filled.sem, av_filled.at(k, b - 1))
                for j in range(4):
                    dve.wait_ge(sc_filled.sem, sc_filled.at(k, 4 * b + j + 1))
                    dve.tensor_tensor(ret[:, b % 2, 4 * j:4 * j + 4],
                                      sc[0:S, j, 0:GT].rearrange("p (h s) -> p h s", h=4),
                                      dmask[:, 4 * j:4 * j + 4], ALU.mult).then_inc(sc_masked.sem, 1)

            turned = pt[0:S, :].rearrange("p (h e) -> p h e", h=H)

            def scale_attn(k, b):
                dve.wait_ge(av_turned.sem, av_turned.at(k, b + 1))
                dve.tensor_scalar(neg[:, b], turned[:, :, HD], -1.0, 1.0, ALU.mult,
                                  ALU.max).then_inc(sums_negated.sem, 1)
                dve.wait_ge(sums_negated.sem, sums_negated.at(k, b + 1))
                dve.scalar_tensor_tensor(den[:, b], turned[:, :, HD], 1.0, neg[:, b], ALU.max,
                                         ALU.max).then_inc(sums_clipped.sem, 1)
                dve.wait_ge(sums_clipped.sem, sums_clipped.at(k, b + 1))
                dve.reciprocal(rec[:, b], den[:, b]).then_inc(sums_inverted.sem, 1)
                dve.wait_ge(sums_inverted.sem, sums_inverted.at(k, b + 1))
                dve.tensor_tensor(att[:, b * H:(b + 1) * H], turned[:, :, 0:HD],
                                  rec[:, b].unsqueeze(2).broadcast_to([S, H, HD]),
                                  ALU.mult).then_inc(att_scaled.sem, 1)

            def wide(t):
                return t[:].unsqueeze(2).broadcast_to([S, GB * H, HD])

            def slot(k, parity, more):
                if more:
                    row_statistics(k + 1, 1 - parity)
                mask_scores(k, 0)
                if more:
                    normalise(k + 1, 1 - parity)
                for b in range(1, GB):
                    mask_scores(k, b)
                    scale_attn(k, b - 1)
                scale_attn(k, GB - 1)
                dve.wait_ge(att_scaled.sem, att_scaled.at(k, GB))
                dve.tensor_reduce(s1[:], att[:], AX.X, ALU.add).then_inc(gn_sum.sem, 1)
                dve.wait_ge(gn_sum.sem, gn_sum.at(k, 1))
                dve.tensor_scalar(mean[:], s1[:], 1.0 / HD, None, ALU.mult).then_inc(gn_mean.sem, 1)
                dve.wait_ge(gn_mean.sem, gn_mean.at(k, 1))
                dve.tensor_tensor(cent[:], att[:], wide(mean), ALU.subtract).then_inc(gn_centred.sem, 1)
                if more:
                    dve.wait_ge(av_filled.sem, av_filled.at(k - 1, GB))
                    read_vg(k + 1, 1 - parity, 0)
                    read_vg(k + 1, 1 - parity, 1)
                dve.wait_ge(gn_squared.sem, gn_squared.at(k, 1))
                dve.tensor_reduce(s2[:], sq[:], AX.X, ALU.add).then_inc(gn_sqsum.sem, 1)
                dve.wait_ge(gn_sqsum.sem, gn_sqsum.at(k, 1))
                dve.tensor_scalar(gveps[:], s2[:], 1.0 / HD, EPS, ALU.mult, ALU.add).then_inc(gn_veps.sem, 1)
                if more:
                    read_vg(k + 1, 1 - parity, 2)
                dve.wait_ge(gate_tanh.sem, gate_tanh.at(k, 1))
                dve.scalar_tensor_tensor(gate[:], th[:], 1.0, z[:, parity], ALU.add,
                                         ALU.mult).then_inc(gate_ready.sem, 1)
                dve.wait_ge(gn_rstd.sem, gn_rstd.at(k, 1))
                dve.tensor_tensor(gn[:].rearrange("p b (h e) -> p (b h) e", h=H), cent[:], wide(grstd),
                                  ALU.mult).then_inc(gn_scaled.sem, 1)
                if more:
                    read_vg(k + 1, 1 - parity, 3)
                dve.wait_ge(gn_shifted.sem, gn_shifted.at(k, 1))
                dve.wait_ge(gate_ready.sem, gate_ready.at(k, 1))
                dve.wait_ge(y_turned.sem, y_turned.at(k, 0))
                dve.tensor_tensor(y[:], gn[:], gate[:], ALU.mult).then_inc(y_ready.sem, 1)
                dve.wait_ge(res_biased.sem, res_biased.at(k, 1))
                dve.wait_ge(x1_stored.sems[parity], x1_stored.done(k - 2, parity))
                for b, bank in zip(range(GB), (pav, pt) * 2):
                    dve.wait_ge(o_filled.sem, o_filled.at(k, b + 1))
                    dve.tensor_tensor(x1[:, parity, b], bank[0:S, 0:E], xb[:, b],
                                      ALU.add).then_inc(x1_ready.sem, 1)

            row_statistics(0, 0)
            dve.wait_ge(weights_loaded.sem, W_ALL)
            dve.wait_ge(decay_exp.sem, H)
            dve.tensor_tensor(dmask[:], dmask[:], causal[:].unsqueeze(1).broadcast_to([S, H, S]),
                              ALU.mult).then_inc(mask_ready.sem, 1)
            normalise(0, 0)
            dve.wait_ge(mask_ready.sem, 1)
            dve.wait_ge(constants.sem, 2)
            for b in range(GB):
                read_vg(0, 0, b)
            for_groups(dve, slot)

        @block.tensor
        def _(pe):
            pe.wait_ge(weights_loaded.sem, W_ALL)
            pe.sem_inc(unit.sem, unit.credit)
            pe.sem_inc(sc_filled.sem, sc_filled.credit)
            pe.sem_inc(av_filled.sem, av_filled.credit)

            def ring_free(k, u):
                if u < 2:
                    pe.wait_ge(dve_read.sem, dve_read.at(k - 1, 6 + 2 * u))
                elif u < 8:
                    pe.wait_ge(act_read.sem, act_read.at(k, u - 1))
                else:
                    pe.wait_ge(dve_read.sem, dve_read.at(k, 2 * (u - 8) + 2))

            def turn_xn(k):
                for c in range(EC):
                    ring_free(k, c)
                    pe.wait_ge(xn_ready.sem, xn_ready.at(k, GB))
                    for b in range(GB):
                        mm = pe.transpose(ring[:, c, b * S:(b + 1) * S], xn[:, b, c * P:(c + 1) * P],
                                          ident[0:S, 0:S])
                    mm.then_inc(unit.sem, 1)

            def project_qk(k):
                pe.wait_ge(act_read.sem, act_read.at(k, EC))
                for w in range(2):
                    for c in range(EC):
                        u = 2 + 2 * w + c
                        ring_free(k, u)
                        for kc in range(EC):
                            mm = pe.matmul(ring[:, u % 2, 0:GT], wqk[:, w, kc, c * P:(c + 1) * P], xnT[:, kc],
                                           start=kc == 0, stop=kc == EC - 1)
                        mm.then_inc(unit.sem, 1)

            def project_vg(k):
                for b in range(GB):
                    u = 6 + b
                    ring_free(k, u)
                    for kc in range(EC):
                        mm = pe.matmul(ring[0:S, u % 2, :], xnT[:, kc, b * S:(b + 1) * S], wvg[:, kc],
                                       start=kc == 0, stop=kc == EC - 1)
                    mm.then_inc(unit.sem, 1)

            def scores(k, parity, b):
                for j in range(4):
                    c = j // 2
                    pe.wait_ge(q_spread.sem, q_spread.at(k, 2 * b + c + 1))
                    pe.wait_ge(sc_masked.sem, sc_masked.at(k, 4 * b + j - 3))
                    pe.matmul(sc[0:S, j, 0:GT], qkT[:, parity, 1, c, b * S:(b + 1) * S],
                              qm[:, b % 2, c, 4 * (j % 2):4 * (j % 2) + 4],
                              start=True, stop=True).then_inc(sc_filled.sem, 1)

            def attend(k, parity, b):
                pe.wait_ge(sc_masked.sem, sc_masked.at(k, 4 * b + 4))
                if b == 0:
                    pe.wait_ge(x1_ready.sem, x1_ready.at(k, 0))
                pe.wait_ge(av_copied.sem, av_copied.at(k, b))
                for q in range(4):
                    for g in range(4):
                        mm = pe.matmul(pav[32 * g:32 * g + 32, q * S:(q + 1) * S], vaug[:, parity, b, 4 * q + g],
                                       ret[:, b % 2, 4 * q + g], start=True, stop=True)
                mm.then_inc(av_filled.sem, 1)

            def turn_attn(k, b):
                pe.wait_ge(av_copied.sem, av_copied.at(k, b + 1))
                pe.wait_ge(att_scaled.sem, att_scaled.at(k, b))
                for q in range(4):
                    mm = pe.transpose(pt[0:S, q * P:(q + 1) * P], av[:, q * S:(q + 1) * S], ident[:])
                mm.then_inc(av_turned.sem, 1)

            def slot(k, parity, more):
                pe.wait_ge(act_read.sem, act_read.at(k, 6))
                scores(k, parity, 0)
                pe.wait_ge(dve_read.sem, dve_read.at(k, 8))
                scores(k, parity, 1)
                attend(k, parity, 0)
                if more:
                    turn_xn(k + 1)
                for b in range(2, GB):
                    turn_attn(k, b - 2)
                    scores(k, parity, b)
                    attend(k, parity, b - 1)
                turn_attn(k, 2)
                attend(k, parity, 3)
                if more:
                    project_qk(k + 1)
                turn_attn(k, 3)
                if more:
                    project_vg(k + 1)
                pe.wait_ge(y_ready.sem, y_ready.at(k, 1))
                pe.wait_ge(att_scaled.sem, att_scaled.at(k, GB))
                for c, bank in enumerate((pav, pt)):
                    for b in range(GB):
                        mm = pe.transpose(bank[:, b * S:(b + 1) * S], y[:, b, c * P:(c + 1) * P], ident[0:S, 0:S])
                    mm.then_inc(y_turned.sem, 1)
                pe.wait_ge(yT_copied.sem, yT_copied.at(k, EC))
                for b, bank in zip(range(GB), (pav, pt) * 2):
                    if b >= 2:
                        pe.wait_ge(x1_ready.sem, x1_ready.at(k, b - 1))
                    for kc in range(EC):
                        mm = pe.matmul(bank[0:S, 0:E], yT[:, kc, b * S:(b + 1) * S], wo[:, kc],
                                       start=kc == 0, stop=kc == EC - 1)
                    mm.then_inc(o_filled.sem, 1)

            turn_xn(0)
            project_qk(0)
            project_vg(0)
            for_groups(pe, slot)


def replicate(a, rows):
    return np.ascontiguousarray(np.broadcast_to(a, (rows,) + a.shape))


def layout_retention(i):
    j = np.arange(S)
    rel = j[None, :] - j[:, None]
    p = np.arange(P)
    return {
        "x": i["x"], "Wq": i["L0_attn_Wq"], "Wk": i["L0_attn_Wk"], "Wv": i["L0_attn_Wv"], "Wg": i["L0_attn_Wg"],
        "Wo": i["L0_attn_Wo"],
        "bq": np.ascontiguousarray(i["L0_attn_bq"].reshape(EC, P).T),
        "bk": np.ascontiguousarray(i["L0_attn_bk"].reshape(EC, P).T),
        "bv": replicate(i["L0_attn_bv"], S), "bg": replicate(i["L0_attn_bg"], S),
        "gn_w": replicate(i["L0_attn_gn_w"], S), "gn_b": replicate(i["L0_attn_gn_b"], S),
        "bo": replicate(i["L0_attn_bo"], S), "decay": replicate(i["L0_attn_decay"], S),
        "rel": np.maximum(rel, 0).astype(np.float32), "causal": (rel >= 0).astype(np.float32),
        "headmask": np.where(p[:, None] // HD == np.arange(8)[None, :], HD ** -0.5, 0).astype(np.float32),
        "ident": np.eye(P, dtype=np.float32),
    }


def rope_tables(length, dim):
    inv = np.float32(1.0) / np.float32(10000.0) ** (np.arange(0, dim, 2, dtype=np.float32) / np.float32(dim))
    f = np.arange(length, dtype=np.float32)[:, None] * inv[None, :]
    return np.repeat(np.sin(f), 2, axis=-1), np.repeat(np.cos(f), 2, axis=-1)


HP = H // 2
MC = H * DQ // P


def phase_query_weights(nc, d, t):
    with ExitStack() as ctx:
        def sb(name, shape, dt=F32):
            return ctx.enter_context(nc.sbuf_tensor("w_" + name, shape, dt))

        def sem(name):
            return ctx.enter_context(nc.semaphore("w_" + name))

        wq = sb("wq", [K, H, E])
        wkcq = sb("wkcq", [K, H, DQ])
        wqr = sb("wqr", [R, H, 3, P])
        wkr = sb("wkr", [R, H, DC])
        bank = ctx.enter_context(nc.psum_tensor("w_bank", [P, 8, 512], F32))
        loaded, filled, copied = sem("loaded"), sem("filled"), sem("copied")
        split = sem("split")
        block = ctx.enter_context(nc.Block())
        N_WC = H * EC

        @block.sync
        def _(sp):
            for dst, src in ((wq[:], d["xWq"].rearrange("(h k) e -> k h e", k=K)),
                             (wkcq[:], d["w_kc_q"].rearrange("h k q -> k h q")),
                             (wqr[:], d["W_qrT"].rearrange("r (h t e) -> r h t e", h=H, t=3)),
                             (wkr[:], d["W_krT"].rearrange("r (h e) -> r h e", h=H)),
                             (t["cosq"][:], d["cosq"]), (t["sinq"][:], d["sinq"])):
                sp.dma_start(dst, src).then_inc(loaded, 16)
            sp.wait_ge(loaded, 16 * 6)

        @block.tensor
        def _(pe):
            pe.wait_ge(loaded, 16 * 6)
            for n in range(N_WC + H):
                if n >= 8:
                    pe.wait_ge(copied, n - 7)
                if n < N_WC:
                    h, c = n // EC, n % EC
                    pe.matmul(bank[:, n % 8, 0:DQ], wq[:, h, c * P:(c + 1) * P], wkcq[:, h],
                              start=True, stop=True).then_inc(filled, 1)
                else:
                    h = n - N_WC
                    for j in range(3):
                        mm = pe.matmul(bank[:, n % 8, j * DC:(j + 1) * DC], wqr[:, h, j], wkr[:, h],
                                       start=True, stop=True)
                    mm.then_inc(filled, 1)

        @block.scalar
        def _(act):
            for n in range(N_WC):
                h, c = n // EC, n % EC
                act.wait_ge(filled, n + 1)
                act.copy(t["wch"][:, c, h * DQ:(h + 1) * DQ], bank[:, n % 8, 0:DQ]).then_inc(split, 1)

        @block.vector
        def _(dve):
            for n in range(N_WC + H):
                h, c = n // EC, n % EC
                dve.wait_ge(filled, n + 1)
                if n < N_WC:
                    dve.wait_ge(split, n + 1)
                    cols = slice(h * DQ, (h + 1) * DQ)
                    dve.tensor_tensor(t["wcl"][:, c, cols], bank[:, n % 8, 0:DQ], t["wch"][:, c, cols].bitcast(F32),
                                      ALU.subtract).then_inc(copied, 1)
                else:
                    dve.tensor_copy(t["ac"][:, n - N_WC],
                                    bank[:, n % 8, 0:3 * DC].rearrange("p (j e) -> p j e", j=3)).then_inc(copied, 1)


def phase_queries(nc, d):
    with ExitStack() as outer:
        t = {n: outer.enter_context(nc.sbuf_tensor("q_" + n, shape, dt)) for n, shape, dt in (
            ("wch", [P, EC, H * DQ], F32R), ("wcl", [P, EC, H * DQ], F32R), ("ac", [P, H, 3, DC], F32),
            ("cosq", [P, 3, S], F32), ("sinq", [P, 3, S], F32))}
        phase_query_weights(nc, d, t)
        wch, wcl, ac, cosq, sinq = (t[n] for n in ("wch", "wcl", "ac", "cosq", "sinq"))
        ctx = outer

        def sb(name, shape, dt=F32):
            return ctx.enter_context(nc.sbuf_tensor("q_" + name, shape, dt))

        def ps(name, shape):
            return ctx.enter_context(nc.psum_tensor("q_" + name, shape, F32))

        def sig(name, each, credit=0):
            return Signal(ctx, nc, "q_" + name, each, credit)

        ident = sb("ident", [P, P])
        mhalf = sb("mhalf", [S, GB])
        x = sb("x", [S, 2, GB, E])
        stats = sb("stats", [S, GB, 6])
        mv = sb("mv", [S, GB, 2])
        veps = sb("veps", [S, GB])
        rstd = sb("rstd", [S, GB])
        xn = sb("xn", [S, GB, E])
        xh = sb("xh", [P, 2, EC, GT], F32R)
        xl = sb("xl", [P, 2, EC, GT], F32R)
        rot = sb("rot", [P, 2, 6, GT])
        qs = sb("qs", [DC, 2, 2, GB, 4, S], F32R)

        pT = ps("pT", [P, EC, 512])
        pq = ps("pq", [P, 4, 512])
        pp = ps("pp", [P, 2, 512])

        ident_loaded = sig("ident_loaded", 0)
        constants = sig("constants_set", 0)
        x_loaded = Transfer(ctx, nc, "q_x_loaded")
        row_stats = sig("row_stats", GB)
        stats_complete = sig("row_stats_complete", 1)
        row_mv = sig("row_mean_var", GB)
        row_veps = sig("row_var_eps", 1)
        row_rstd = sig("row_rstd", 1)
        xn_ready = sig("xn_ready", GB, 2 * GB)
        xn_turned = sig("xn_turned", EC, EC)
        x_high = sig("x_high_ready", EC)
        x_low = sig("x_low_ready", EC, EC)
        q_filled = sig("q_filled", MC, 2 * MC)
        q_rotated = sig("q_rotated", MC, 4)
        p_filled = sig("q_absorbed", HP, 2)
        p_high = sig("q_high_ready", HP)
        p_low = sig("q_low_ready", HP, 2)
        stored = [Signal(ctx, nc, f"q_stored{i}", 64) for i in range(2)]
        block = ctx.enter_context(nc.Block())

        @block.sync
        def _(sp):
            def load(k, parity):
                sp.wait_ge(xn_ready.sem, xn_ready.at(k - 2, GB))
                src = d["x1"][bass.ds(k * GB, GB)].rearrange("b s e -> s b e")
                sp.dma_start(x[:, parity], src).then_inc(x_loaded.sems[parity], 16)

            def slot(k, parity, more):
                if more:
                    load(k + 1, 1 - parity)
                for r in range(4):
                    buf = r % 2
                    sp.wait_ge(p_low.sem, p_low.at(k, 2 * r + 2))
                    for part in range(2):
                        dst = d["qp"][bass.ds(k * GB, GB), part, :, 4 * r * S:4 * (r + 1) * S]
                        sp.dma_start(dst.rearrange("b e n -> e b n"),
                                     qs[:, buf, part].bitcast(F32).rearrange("e b h s -> e b (h s)")
                                     ).then_inc(stored[buf].sem, 16)

            sp.dma_start(ident[:], d["ident"]).then_inc(ident_loaded.sem, 16)
            load(0, 0)
            for_groups(sp, slot)
            for buf in range(2):
                sp.wait_ge(stored[buf].sem, stored[buf].at(NG - 1, 64))

        @block.gpsimd
        def _(pool):
            pool.memset(mhalf[:], -0.5).then_inc(constants.sem, 1)
            pool.wait_ge(constants.sem, 1)

            def rows_rstd(k):
                pool.wait_ge(row_veps.sem, row_veps.at(k, 1))
                pool.tensor_tensor(rstd[:], veps[:], mhalf[:], ALU.pow).then_inc(row_rstd.sem, 1)

            def slot(k, parity, more):
                if more:
                    rows_rstd(k + 1)

            rows_rstd(0)
            for_groups(pool, slot)

        @block.scalar
        def _(act):
            def copy_high(k, parity):
                act.wait_ge(q_filled.sem, q_filled.at(k - 2, MC))
                for c in range(EC):
                    act.wait_ge(xn_turned.sem, xn_turned.at(k, c + 1))
                    act.copy(xh[:, parity, c], pT[:, c, 0:GT]).then_inc(x_high.sem, 1)

            def slot(k, parity, more):
                for p in range(HP):
                    buf = (p // 2) % 2
                    if p % 2 == 0:
                        act.wait_ge(stored[buf].sem, stored[buf].at(k, 32 * (p // 4)))
                    act.wait_ge(p_filled.sem, p_filled.at(k, p + 1))
                    for side in range(2):
                        cp = act.copy(qs[:, buf, 0, :, 2 * (p % 2) + side],
                                      pp[DC * side:DC * side + DC, p % 2, 0:GT].rearrange("e (b s) -> e b s", b=GB))
                    cp.then_inc(p_high.sem, 1)
                    if p == 4 and more:
                        copy_high(k + 1, 1 - parity)

            copy_high(0, 0)
            for_groups(act, slot)

        @block.vector
        def _(dve):
            dve.sem_inc(xn_ready.sem, xn_ready.credit)
            dve.sem_inc(x_low.sem, x_low.credit)
            dve.sem_inc(q_rotated.sem, q_rotated.credit)
            dve.sem_inc(p_low.sem, p_low.credit)

            def row_statistics(k, parity):
                dve.wait_ge(x_loaded.sems[parity], x_loaded.done(k, parity))
                for b in range(GB):
                    dve.bn_stats(stats[:, b], x[:, parity, b]).then_inc(row_stats.sem, 1)
                dve.wait_ge(row_stats.sem, row_stats.at(k, GB))
                dve.sem_inc(stats_complete.sem, 1)
                for b in range(GB):
                    dve.bn_aggr(mv[:, b], stats[:, b]).then_inc(row_mv.sem, 1)
                dve.wait_ge(row_mv.sem, row_mv.at(k, GB))
                dve.tensor_scalar(veps[:], mv[:, :, 1], EPS, None, ALU.add).then_inc(row_veps.sem, 1)

            def normalise(k, parity):
                dve.wait_ge(row_rstd.sem, row_rstd.at(k, 1))
                dve.wait_ge(xn_turned.sem, xn_turned.at(k - 1, EC))
                for b in range(GB):
                    dve.tensor_scalar(xn[:, b], x[:, parity, b], mv[:, b, 0:1], rstd[:, b:b + 1],
                                      ALU.subtract, ALU.mult).then_inc(xn_ready.sem, 1)

            def split_low(k, parity):
                dve.wait_ge(q_filled.sem, q_filled.at(k - 2, MC))
                for c in range(EC):
                    dve.wait_ge(x_high.sem, x_high.at(k, c + 1))
                    dve.tensor_tensor(xl[:, parity, c], pT[:, c, 0:GT], xh[:, parity, c].bitcast(F32),
                                      ALU.subtract).then_inc(x_low.sem, 1)

            def table(t, c, rows):
                return t[rows, c].unsqueeze(1).broadcast_to([rows.stop - rows.start, GB, S])

            def rotate(k, p):
                full, top, bottom = slice(0, P), slice(0, DC), slice(DC, P)
                steps = (((full, cosq, full, 0), (full, sinq, full, 1)),
                         ((top, cosq, top, 2), (top, sinq, bottom, 2), (bottom, cosq, top, 5), (bottom, sinq, bottom, 5)),
                         ((full, cosq, full, 3), (full, sinq, full, 4)))
                dve.wait_ge(p_filled.sem, p_filled.at(k, p - 1))
                for c, ops in enumerate(steps):
                    m = 3 * p + c
                    dve.wait_ge(q_filled.sem, q_filled.at(k, m + 1))
                    for rows, tab, to, place in ops:
                        mul = dve.tensor_tensor(
                            rot[to, p % 2, place].rearrange("e (b s) -> e b s", b=GB),
                            pq[rows, m % 4, 0:GT].rearrange("e (b s) -> e b s", b=GB), table(tab, c, rows), ALU.mult)
                    mul.then_inc(q_rotated.sem, 1)

            def low(k, p):
                buf = (p // 2) % 2
                dve.wait_ge(p_high.sem, p_high.at(k, p + 1))
                for side in range(2):
                    head = 2 * (p % 2) + side
                    sub = dve.tensor_tensor(qs[:, buf, 1, :, head],
                                            pp[DC * side:DC * side + DC, p % 2, 0:GT].rearrange("e (b s) -> e b s", b=GB),
                                            qs[:, buf, 0, :, head].bitcast(F32), ALU.subtract)
                sub.then_inc(p_low.sem, 1)

            def slot(k, parity, more):
                for p in range(HP):
                    rotate(k, p)
                    if p >= 1:
                        low(k, p - 1)
                    if p == 1 and more:
                        row_statistics(k + 1, 1 - parity)
                    if p == 2 and more:
                        normalise(k + 1, 1 - parity)
                    if p == 6 and more:
                        split_low(k + 1, 1 - parity)
                low(k, HP - 1)

            row_statistics(0, 0)
            normalise(0, 0)
            split_low(0, 0)
            for_groups(dve, slot)

        @block.tensor
        def _(pe):
            pe.wait_ge(ident_loaded.sem, 16)
            pe.sem_inc(xn_turned.sem, xn_turned.credit)
            pe.sem_inc(q_filled.sem, q_filled.credit)
            pe.sem_inc(p_filled.sem, p_filled.credit)

            def turn_xn(k):
                pe.wait_ge(xn_ready.sem, xn_ready.at(k, GB))
                pe.wait_ge(x_low.sem, x_low.at(k - 1, EC))
                for c in range(EC):
                    for b in range(GB):
                        mm = pe.transpose(pT[:, c, b * S:(b + 1) * S], xn[:, b, c * P:(c + 1) * P], ident[0:S, 0:S])
                    mm.then_inc(xn_turned.sem, 1)

            def project(k, parity, m):
                pe.wait_ge(q_rotated.sem, q_rotated.at(k, m - 3))
                cols = slice(m * P, (m + 1) * P)
                terms = [(w, xx, kc) for w, xx in ((wch, xh), (wch, xl), (wcl, xh)) for kc in range(EC)]
                for n, (w, xx, kc) in enumerate(terms):
                    mm = pe.matmul(pq[:, m % 4, 0:GT], w[:, kc, cols], xx[:, parity, kc],
                                   start=n == 0, stop=n == len(terms) - 1)
                mm.then_inc(q_filled.sem, 1)

            def absorb(k, p):
                pe.wait_ge(q_rotated.sem, q_rotated.at(k, 3 * p + 3))
                pe.wait_ge(p_low.sem, p_low.at(k, p - 1))
                for j in range(3):
                    for side in range(2):
                        mm = pe.matmul(pp[DC * side:DC * side + DC, p % 2, 0:GT], ac[:, 2 * p + side, j],
                                       rot[:, p % 2, 3 * side + j], start=j == 0, stop=j == 2)
                mm.then_inc(p_filled.sem, 1)

            def slot(k, parity, more):
                pe.wait_ge(x_low.sem, x_low.at(k, EC))
                for p in range(HP):
                    for c in range(3):
                        project(k, parity, 3 * p + c)
                    if p >= 1:
                        absorb(k, p - 1)
                    if p == 3 and more:
                        turn_xn(k + 1)
                absorb(k, HP - 1)

            turn_xn(0)
            for_groups(pe, slot)


def layout_queries(i):
    wqr = i["L0_xattn_W_qr"]
    cols = []
    for h in range(H):
        e = np.arange(P) if h % 2 == 0 else np.arange(DC, DQ)
        rest = np.arange(P, DQ) if h % 2 == 0 else np.arange(DC)
        rows = np.concatenate([e, (e + DQ // 2) % DQ, rest, (rest + DQ // 2) % DQ])
        cols.append(wqr[h][rows].T)
    sin, cos = rope_tables(S, DQ)
    e = np.arange(DQ)
    turned = (sin[:, (e + DQ // 2) % DQ] * np.where(e < DQ // 2, 1, -1)).astype(np.float32)

    def by_chunk(t):
        return np.ascontiguousarray(np.concatenate([t, t], 1).T.reshape(3, P, S).transpose(1, 0, 2)).astype(np.float32)

    return {
        "xWq": i["L0_xattn_Wq"], "w_kc_q": i["L0_xattn_w_kc_q"],
        "W_qrT": np.ascontiguousarray(np.concatenate(cols, 1)),
        "W_krT": np.ascontiguousarray(np.transpose(i["L0_xattn_W_kr"], (2, 0, 1)).reshape(R, H * DC)),
        "cosq": by_chunk(cos), "sinq": by_chunk(turned), "ident": np.eye(P, dtype=np.float32),
    }


LC = 12
LP = -(-L // LC)
LFULL = L // LC
LREST = L - LFULL * LC
QROWS = H * S
MR = -(-QROWS // 13)
MR += MR % 2
MB = -(-QROWS // MR)
HALF = QROWS // 2
BANK = HALF // 2
PR = 4


def rows_of(c):
    return LFULL + (1 if c < LREST else 0)


def start_of(c):
    return c * LFULL + min(c, LREST)


def block_rows(r):
    return min(MR, QROWS - r * MR)


def wait(eng, sem, value):
    if not (isinstance(value, int) and value <= 0):
        eng.wait_ge(sem, value)


class Ring:

    def __init__(self, ctx, nc, name, units, last_units, last):
        self.index = {u: n for n, u in enumerate(units)}
        self.last_index = {u: n for n, u in enumerate(last_units)}
        self.last = last
        self.each = len(units) // 2
        assert len(units) % 2 == 0
        self.filled = [ctx.enter_context(nc.semaphore(f"{name}_filled{i}")) for i in range(2)]
        self.read = [ctx.enter_context(nc.semaphore(f"{name}_read{i}")) for i in range(2)]

    def place(self, n, unit):
        if isinstance(n, int) and n >= self.last:
            i = self.last_index[(n,) + unit]
            return i % 2, (self.last + 1) * self.each + i // 2 + 1
        i = self.index[unit]
        return i % 2, n * self.each + (self.each + i // 2 + 1)


def phase_cross_attention(nc, d):
    with ExitStack() as ctx:
        def sb(name, shape, dt=F32):
            return ctx.enter_context(nc.sbuf_tensor("x_" + name, shape, dt))

        def ps(name, shape):
            return ctx.enter_context(nc.psum_tensor("x_" + name, shape, F32))

        def sig(name, each, credit=0):
            return Signal(ctx, nc, "x_" + name, each, credit)

        def transfer(name, amount, credit=0):
            return Transfer(ctx, nc, "x_" + name, credit, amount)

        ident = sb("ident", [P, P])
        cosk = sb("cosk", [LP, LC, DC])
        sink = sb("sink", [LP, LC, DC])
        ones = sb("ones", [P, DC])
        wkc = sb("wkc", [K, H, DC])
        woT = sb("woT", [K, H, E])
        wco = sb("wco", [P, H // 2, E])
        raw = sb("raw", [LP, 2, LC, DC])
        t1 = sb("t1", [LP, LC, DC])
        t2 = sb("t2", [LP, LC, DC])
        rotated = sb("rotated", [LP, LC, DC])
        kv = sb("kv", [LP, 2, LC, DC])
        ks = sb("ks", [LP, LC, 2 * DC])
        ka = sb("ka", [P, 2, L], F32R)
        kb = sb("kb", [P, 2, L], F32R)
        qa = sb("qa", [P, 2, QROWS], F32R)
        qb = sb("qb", [P, 2, QROWS], F32R)
        mx = sb("mx", [MR, MB, 3])
        negm = sb("negm", [MR, MB])
        mrow = sb("mrow", [MB, MR], F32R)
        prob = sb("prob", [LP, PR, QROWS])
        acc = sb("acc", [LP, 2, QROWS])
        ctxs = sb("ctxs", [P, 2, BANK])
        rden = sb("rden", [P, 2, BANK])
        ctxn = sb("ctxn", [P, 2, BANK])
        xr = sb("xr", [S, 2, E])
        x2 = sb("x2", [S, 2, E])

        psc = ps("scores", [P, 2, 2, 512])
        pav = ps("context", [P, 2, 512])
        ring = ps("ring", [P, 2, 512])

        PIECES = 6
        C_M = 10
        side = {(c, i): [] for c in range(LC) for i in range(PIECES)}
        for place, u in (((2, 0), ("kvT", 0)), ((2, 3), ("kvT", 1)), ((3, 0), ("kvT", 2)), ((C_M, 1), ("mT",)),
                         ((C_M, 2), ("den", 0)), ((C_M, 4), ("den", 1)), ((0, 4), ("out",))):
            side[place].append(u)
        for m in range(3 * MB):
            place = 3 * PIECES + 2 + m
            side[place // PIECES, place % PIECES].append(("max", m // 3, m % 3))
        beside = {c: [u for i in range(PIECES) for u in side[c, i]] for c in range(LC)}
        units = [u for c in range(LC) for u in beside[c]]
        ends = [("out",), ("den", 0), ("den", 1)]
        rg = Ring(ctx, nc, "x_ring", units, [(n,) + u for n in (B - 1, B, B + 1) for u in ends], B - 1)

        loaded = sig("weights_loaded", 0)
        memset = sig("memset", 0)
        rows_zeroed = sig("rows_zeroed", 0)
        wco_filled = sig("wco_filled", 0)
        wco_copied = sig("wco_copied", 0)
        q_loaded = transfer("q_loaded", 48)
        kv_loaded = transfer("kv_loaded", 32)
        xr_loaded = transfer("xr_loaded", 16, 16)
        m_stored = transfer("m_stored", 16)
        m_loaded = transfer("m_loaded", 16)
        x2_stored = transfer("x2_stored", 16, 32)
        rope_terms = sig("rope_terms", 3, 3)
        kv_roped = sig("kv_roped", 1, 1)
        kv_kept = sig("kv_kept", 1, 1)
        kv_high = sig("kv_high", 1, 1)
        kv_low = sig("kv_low", 1, 1)
        max_ready = sig("maxima_ready", 1, 1)
        ctx_normed = sig("context_normed", 2, 2)
        s_filled = sig("scores_filled", 2 * LC)
        exp_done = sig("exp_done", 2 * LC, 2)
        av_done = sig("context_added", LC, 3)
        acc_done = sig("sums_added", LC - 1, 3)
        ctx_saved = sig("context_saved", 1)

        span = [(start_of(4 * i), start_of(4 * i + 3) + rows_of(4 * i + 3)) for i in range(3)]
        block = ctx.enter_context(nc.Block())
        N_W, N_MEMSET = 5, 8

        def in_turn(eng, slot):
            slot(-1, 1, True)
            slot(0, 0, True)
            with eng.Fori(0, (B - 2) // 2) as i:
                for parity in (1, 0):
                    slot(i * 2 + (2 - parity), parity, True)
            slot(B - 1, 1, False)

        def is_at(n, value):
            return isinstance(n, int) and n == value

        @block.sync
        def _(sp):
            for dst, src in ((ident[:], d["ident"]), (cosk[:], d["cosk"]), (sink[:], d["sink"]),
                             (wkc[:], d["w_kc_kv"].rearrange("h k e -> k h e")),
                             (woT[:], d["xWoT"].rearrange("(h k) e -> k h e", k=K))):
                sp.dma_start(dst, src).then_inc(loaded.sem, 16)
            sp.wait_ge(memset.sem, N_MEMSET)

            def load_kv(n, parity):
                wait(sp, kv_roped.sem, kv_roped.at(n - 3, 1))
                rows = d["ctx"][bass.ds(n, 1)].rearrange("b l e -> (b l) e")
                sp.dma_start(raw[0:LFULL, parity].rearrange("p c e -> p (c e)"),
                             rows[0:LFULL * LC].rearrange("(p c) e -> p (c e)", c=LC)).then_inc(kv_loaded.sems[parity], 16)
                sp.dma_start(raw[LFULL:LP, parity, 0:LREST].rearrange("p c e -> p (c e)"),
                             rows[LFULL * LC:L].rearrange("(p c) e -> p (c e)", c=LREST)
                             ).then_inc(kv_loaded.sems[parity], 16)

            def load_q(n, parity):
                wait(sp, s_filled.sem, s_filled.at(n - 1, 0))
                for dst, part in ((qa[0:DC], 0), (qa[DC:P], 0), (qb[0:DC], 1)):
                    sp.dma_start(dst[:, parity].bitcast(F32),
                                 d["qp"][bass.ds(n, 1), part].rearrange("b e n -> (b e) n")
                                 ).then_inc(q_loaded.sems[parity], 16)

            def load_xr(n, parity):
                bank, value = rg.place(n, ("out",))
                wait(sp, rg.read[bank], value)
                sp.dma_start(xr[:, parity], d["x1"][bass.ds(n, 1)].rearrange("b s e -> (b s) e")
                             ).then_inc(xr_loaded.sems[parity], 16)

            def store_x2(n, parity):
                bank, value = rg.place(n + 2, ("out",))
                sp.wait_ge(rg.read[bank], value)
                sp.dma_start(d["x2"][bass.ds(n, 1)].rearrange("b s e -> (b s) e"), x2[:, parity]
                             ).then_inc(x2_stored.sems[parity], 16)

            def load_m(n, parity):
                bank, value = rg.place(n - 1, ("mT",))
                sp.wait_ge(rg.read[bank], value)
                sp.dma_start(d["m"][parity], mrow[:].bitcast(F32)).then_inc(m_stored.sems[parity], 16)
                sp.wait_ge(m_stored.sems[parity], m_stored.done(n, parity))
                sp.dma_start(qb[DC:DC + 1, parity].bitcast(F32),
                             d["m"][parity].rearrange("r m -> (r m)")[0:QROWS].unsqueeze(0)
                             ).then_inc(m_loaded.sems[parity], 16)

            def slot(n, parity, store, kv_too=True):
                if kv_too:
                    load_kv(n + 2, parity)
                load_q(n + 1, 1 - parity)
                load_xr(n, parity)
                if store:
                    store_x2(n - 2, parity)
                load_m(n + 1, 1 - parity)

            for parity in range(2):
                sp.sem_inc(x2_stored.sems[parity], x2_stored.credit)
                sp.sem_inc(xr_loaded.sems[parity], xr_loaded.credit)
            load_q(0, 0)
            load_kv(0, 0)
            load_kv(1, 1)
            load_m(0, 0)
            slot(0, 0, False)
            slot(1, 1, False)
            with sp.Fori(1, (B - 2) // 2) as i:
                for parity in range(2):
                    slot(i * 2 + parity, parity, True)
            slot(B - 2, 0, True, False)
            load_xr(B - 1, 1)
            store_x2(B - 3, 1)
            store_x2(B - 2, 0)
            store_x2(B - 1, 1)
            for parity in range(2):
                sp.wait_ge(x2_stored.sems[parity], x2_stored.done(B - 2 + parity, parity))

        @block.gpsimd
        def _(pool):
            for t, v in ((ones[:], 1.0), (raw[:], 0.0), (acc[:], 1.0), (ctxs[:], 0.0), (xr[:], 0.0), (ctxn[:], 0.0), (mx[:], 0.0)):
                pool.memset(t, v).then_inc(memset.sem, 1)
            pool.sem_inc(acc_done.sem, acc_done.credit)
            pool.wait_ge(memset.sem, N_MEMSET)

            def slot(n, parity, more):
                if is_at(n, -1):
                    return
                bank, value = rg.place(n - 1, ("den", 1))
                pool.wait_ge(rg.filled[bank], value)
                for c in range(1, LC):
                    rows = rows_of(c)
                    pool.wait_ge(exp_done.sem, exp_done.at(n, 2 * c + 2))
                    first = prob[0:rows, 0] if c == 1 else acc[0:rows, parity]
                    if c > 1:
                        pool.wait_ge(acc_done.sem, acc_done.at(n, c - 1))
                    pool.tensor_tensor(acc[0:rows, parity], first, prob[0:rows, c % PR],
                                       ALU.add).then_inc(acc_done.sem, 1)

            in_turn(pool, slot)

        @block.scalar
        def _(act):
            act.sem_inc(exp_done.sem, exp_done.credit)

            def exponentials(n, c, u):
                rows = rows_of(c)
                if u == 0:
                    act.wait_ge(av_done.sem, av_done.at(n, c - 3))
                    act.wait_ge(acc_done.sem, acc_done.at(n, max(c - 4, 1) if c >= PR else c - 3))
                act.wait_ge(s_filled.sem, s_filled.at(n, 2 * c + u + 1))
                act.activation(prob[0:rows, c % PR, u * HALF:(u + 1) * HALF].rearrange("p (j s) -> p j s", j=2),
                               psc[0:rows, u, :, 0:BANK], ACT.Exp).then_inc(exp_done.sem, 1)

            def copy_turned(n, parity, i):
                if i == 0:
                    wait(act, s_filled.sem, s_filled.at(n, 0))
                bank, value = rg.place(n, ("kvT", i))
                act.wait_ge(rg.filled[bank], value)
                a, b = span[i]
                act.copy(ka[:, parity, a:b], ring[:, bank, 0:b - a])
                act.copy(kb[0:DC, parity, a:b], ring[0:DC, bank, 0:b - a]).then_inc(rg.read[bank], 1)

            def save_context(n):
                act.wait_ge(av_done.sem, av_done.at(n, 0))
                act.wait_ge(ctx_normed.sem, ctx_normed.at(n - 1, 2))
                act.copy(ctxs[:], pav[:, :, 0:BANK]).then_inc(ctx_saved.sem, 1)

            def slot(n, parity, more):
                for c in range(LC):
                    if c == 1 and not is_at(n, -1) and not is_at(n, 0):
                        save_context(n)
                    for u in range(2):
                        if not is_at(n, -1):
                            exponentials(n, c, u)
                        if 2 * c + u in (4, 5, 6) and more:
                            copy_turned(n, 1 - parity, 2 * c + u - 4)
                    if c == 0 and more:
                        act.wait_ge(kv_roped.sem, kv_roped.at(n, 1))
                        bank, value = rg.place(n - 1, ("kvT", 2))
                        wait(act, rg.filled[bank], value)
                        act.copy(ks[:, :, 0:DC].bitcast(F32R), rotated[:]).then_inc(kv_high.sem, 1)
                    if c == 1 and more:
                        wait(act, av_done.sem, av_done.at(n, 0))
                        act.copy(kv[:, 1 - parity], rotated[:]).then_inc(kv_kept.sem, 1)

            in_turn(act, slot)
            save_context(B)

        @block.vector
        def _(dve):
            for t in (kb, qb):
                dve.memset(t[DC:P].bitcast(F32), 0.0).then_inc(rows_zeroed.sem, 1)
            dve.wait_ge(rows_zeroed.sem, 2)
            dve.memset(kb[DC:DC + 1].bitcast(F32), 1.0).then_inc(memset.sem, 1)
            dve.wait_ge(memset.sem, N_MEMSET)

            def rope(n, parity):
                dve.wait_ge(kv_loaded.sems[parity], kv_loaded.done(n + 1, parity))
                half = DC // 2
                dve.tensor_tensor(t1[:], raw[:, parity], cosk[:], ALU.mult).then_inc(rope_terms.sem, 1)
                for to, frm in ((slice(0, half), slice(half, DC)), (slice(half, DC), slice(0, half))):
                    dve.tensor_tensor(t2[:, :, to], raw[:, parity, :, frm], sink[:, :, to],
                                      ALU.mult).then_inc(rope_terms.sem, 1)
                wait(dve, kv_kept.sem, kv_kept.at(n - 1, 1))
                dve.wait_ge(rope_terms.sem, rope_terms.at(n, 3))
                dve.tensor_tensor(rotated[:], t1[:], t2[:], ALU.add).then_inc(kv_roped.sem, 1)
                dve.wait_ge(kv_high.sem, kv_high.at(n, 1))
                dve.tensor_tensor(ks[:, :, DC:2 * DC].bitcast(F32R), rotated[:], ks[:, :, 0:DC],
                                  ALU.subtract).then_inc(kv_low.sem, 1)

            def normalise(n, j):
                bank, value = rg.place(n, ("den", j))
                dve.wait_ge(rg.filled[bank], value)
                if j == 0:
                    wait(dve, ctx_saved.sem, ctx_saved.at(n, 0))
                dve.reciprocal(rden[:, j], ring[:, bank, 0:BANK]).then_inc(rg.read[bank], 1)
                dve.wait_ge(rg.read[bank], value)
                before, value = rg.place(n, ("out",))
                dve.wait_ge(rg.filled[before], value)
                dve.tensor_tensor(ctxn[:, j], ctxs[:, j], rden[:, j], ALU.mult).then_inc(ctx_normed.sem, 1)

            def output(n, parity):
                bank, value = rg.place(n, ("out",))
                dve.wait_ge(rg.filled[bank], value)
                wait(dve, xr_loaded.sems[parity], xr_loaded.done(n - 2, parity))
                wait(dve, x2_stored.sems[parity], x2_stored.done(n - 4, parity))
                dve.tensor_tensor(x2[:, parity], ring[0:S, bank, 0:E], xr[:, parity],
                                  ALU.add).then_inc(rg.read[bank], 1)

            def maximum(n, r, i):
                bank, value = rg.place(n, ("max", r, i))
                dve.wait_ge(rg.filled[bank], value)
                a, b = span[i]
                dve.tensor_reduce(mx[0:block_rows(r), r, i:i + 1], ring[0:block_rows(r), bank, 0:b - a], AX.X,
                                  ALU.max).then_inc(rg.read[bank], 1)

            def slot(n, parity, more):
                for c in range(LC):
                    if c == 0 and more:
                        rope(n, 1 - parity)
                    for u in beside[c]:
                        if u[0] == "den":
                            normalise(n, u[1])
                        elif u[0] == "out":
                            output(n, parity)
                        elif u[0] == "max" and more:
                            maximum(n, u[1], u[2])
                        elif u[0] == "mT" and more:
                            bank, value = rg.place(n, u)
                            dve.wait_ge(rg.filled[bank], value)
                            dve.tensor_copy(mrow[:], ring[0:MB, bank, 0:MR]).then_inc(rg.read[bank], 1)
                    if c == C_M - 1 and more:
                        for i in (1, 2):
                            bank, value = rg.place(n, ("max", MB - 1, i))
                            dve.wait_ge(rg.read[bank], value)
                        dve.tensor_reduce(negm[:], mx[:], AX.X, ALU.max, negate=True).then_inc(max_ready.sem, 1)

            for h in range(H // 2):
                dve.wait_ge(wco_filled.sem, h + 1)
                dve.tensor_copy(wco[:, h], ring[:, h % 2, 0:E]).then_inc(wco_copied.sem, 1)
            in_turn(dve, slot)
            output(B, 0)
            for j in range(2):
                normalise(B, j)
            output(B + 1, 1)

        @block.tensor
        def _(pe):
            pe.wait_ge(loaded.sem, 16 * N_W)
            pe.wait_ge(memset.sem, N_MEMSET)
            pe.sem_inc(av_done.sem, av_done.credit)
            for h in range(H // 2):
                wait(pe, wco_copied.sem, h - 1)
                for s in range(2):
                    mm = pe.matmul(ring[DC * s:DC * s + DC, h % 2, 0:E], wkc[:, h + s * (H // 2)],
                                   woT[:, h + s * (H // 2)], start=True, stop=True)
                mm.then_inc(wco_filled.sem, 1)
            pe.wait_ge(wco_copied.sem, H // 2)

            def scores(n, parity, c, u, j):
                rows, a = rows_of(c), start_of(c)
                cols = slice(u * HALF + j * BANK, u * HALF + (j + 1) * BANK)
                out = psc[0:rows, u, j, 0:BANK]
                if j == 0:
                    pe.wait_ge(exp_done.sem, exp_done.at(n, 2 * c + u - 1))
                pe.matmul(out, ka[:, parity, a:a + rows], qa[:, parity, cols], start=True, stop=False)
                if c == 0 and u == 0 and j == 0:
                    pe.wait_ge(m_loaded.sems[parity], m_loaded.done(n, parity))
                mm = pe.matmul(out, kb[:, parity, a:a + rows], qb[:, parity, cols], start=False, stop=True)
                if j == 1:
                    mm.then_inc(s_filled.sem, 1)

            def context(n, parity, c, j):
                rows = rows_of(c)
                if j == 0:
                    pe.wait_ge(exp_done.sem, exp_done.at(n, 2 * c + 2))
                if c == 0 and j == 0:
                    wait(pe, ctx_saved.sem, ctx_saved.at(n, 0))
                for s in range(2):
                    cols = slice(s * HALF + j * BANK, s * HALF + (j + 1) * BANK)
                    mm = pe.matmul(pav[DC * s:DC * s + DC, j, 0:BANK], kv[0:rows, parity, c],
                                   prob[0:rows, c % PR, cols], start=c == 0, stop=c == LC - 1)
                if j == 1:
                    mm.then_inc(av_done.sem, 1)

            def piece(n, parity, c, i):
                if i % 3 < 2:
                    scores(n, parity, c, i // 3, i % 3)
                elif c >= 1:
                    context(n, parity, c - 1, i // 3)
                elif not is_at(n, 0):
                    context(n - 1, 1 - parity, LC - 1, i // 3)

            def make(n, parity, u):
                bank, value = rg.place(n, u)
                wait(pe, rg.read[bank], value - 1)
                if u[0] == "kvT":
                    pe.wait_ge(kv_low.sem, kv_low.at(n, 1))
                    a = span[u[1]][0]
                    for c in range(4 * u[1], 4 * u[1] + 4):
                        rows, b = rows_of(c), start_of(c) - a
                        mm = pe.transpose(ring[:, bank, b:b + rows], ks[0:rows, c], ident[0:rows, 0:rows])
                elif u[0] == "den":
                    wait(pe, acc_done.sem, acc_done.at(n, 0))
                    for s in range(2):
                        cols = slice(s * HALF + u[1] * BANK, s * HALF + (u[1] + 1) * BANK)
                        mm = pe.matmul(ring[DC * s:DC * s + DC, bank, 0:BANK], ones[0:LP], acc[:, 1 - parity, cols],
                                       start=True, stop=True)
                elif u[0] == "out":
                    wait(pe, ctx_normed.sem, ctx_normed.at(n - 1, 2))
                    for h in range(H // 2):
                        mm = pe.matmul(ring[0:S, bank, 0:E], ctxn[:, h // 4, (h % 4) * S:(h % 4 + 1) * S],
                                       wco[:, h], start=h == 0, stop=h == H // 2 - 1)
                elif u[0] == "max":
                    if u[1] == 0 and u[2] == 0:
                        pe.wait_ge(q_loaded.sems[1 - parity], q_loaded.done(n + 1, 1 - parity))
                    a, b = span[u[2]]
                    r = u[1]
                    mm = pe.matmul(ring[0:block_rows(r), bank, 0:b - a],
                                   qa[:, 1 - parity, r * MR:r * MR + block_rows(r)], ka[:, 1 - parity, a:b],
                                   start=True, stop=True)
                else:
                    pe.wait_ge(max_ready.sem, max_ready.at(n, 1))
                    mm = pe.transpose(ring[0:MB, bank, 0:MR], negm[:], ident[0:MR, 0:MR])
                mm.then_inc(rg.filled[bank], 1)

            def slot(n, parity, more):
                for c in range(LC):
                    for i in range(PIECES):
                        if not is_at(n, -1):
                            piece(n, parity, c, i)
                        for u in side[c, i]:
                            if more or u[0] in ("den", "out"):
                                make(n, parity, u)

            in_turn(pe, slot)
            for j in range(2):
                context(B - 1, 1, LC - 1, j)
            for u in ends:
                make(B, 0, u)
            make(B + 1, 1, ("out",))


def layout_cross(i):
    sin, cos = rope_tables(L, DC)
    half = DC // 2
    sin = np.concatenate([-sin[:, :half], sin[:, half:]], 1)

    def by_row(t):
        padded = np.concatenate([t, np.zeros((LP * LC - L, DC), np.float32)])
        out = padded[:LFULL * LC].reshape(LFULL, LC, DC)
        last = np.zeros((1, LC, DC), np.float32)
        last[0, :LREST] = t[LFULL * LC:]
        return np.ascontiguousarray(np.concatenate([out, last])).astype(np.float32)

    return {"ctx": i["ctx_512"], "cosk": by_row(cos), "sink": by_row(sin), "w_kc_kv": i["L0_xattn_w_kc_kv"],
            "xWoT": np.ascontiguousarray(i["L0_xattn_Wo"].T), "ident": np.eye(P, dtype=np.float32)}


FC = 6
FM = -(-F // FC)
FW_EPS = 1e-8


def hidden_rows(m):
    return min(FM, F - m * FM)


def phase_ffn(nc, d):
    with ExitStack() as ctx:
        def sb(name, shape, dt=F32):
            return ctx.enter_context(nc.sbuf_tensor("f_" + name, shape, dt))

        def ps(name, shape):
            return ctx.enter_context(nc.psum_tensor("f_" + name, shape, F32))

        def sig(name, each, credit=0):
            return Signal(ctx, nc, "f_" + name, each, credit)

        ident = sb("ident", [P, P])
        ones = sb("ones", [P, P])
        mhalf = sb("mhalf", [S, GB])
        w = [sb("w1", [P, EC, F]), sb("w2", [P, EC, F]), sb("w3", [P, FC, E])]
        above = sb("above", [P, FC * E])
        below = sb("below", [P, FC * E])
        t12 = sb("t12", [P, 2, EC, F], F32R)
        t3 = sb("t3", [P, FC, E], F32R)
        part = sb("part", [P, 3, 24])
        total = sb("total", [P, 3])
        mean = sb("mean", [P, 3])
        thr = sb("thr", [P, 3])
        nthr = sb("nthr", [P, 3])
        x = sb("x", [S, 2, GB, E])
        stats = sb("stats", [S, GB, 6])
        mv = sb("mv", [S, GB, 2])
        veps = sb("veps", [S, GB])
        rstd = sb("rstd", [S, GB])
        xn = sb("xn", [S, GB, E])
        xh = sb("xh", [P, 2, EC, GT], F32R)
        xl = sb("xl", [P, 2, EC, GT], F32R)
        th = sb("th", [FM, 2, GT])
        hid = sb("hid", [FM, 2, GT])
        hh = sb("hh", [FM, FC, GT], F32R)
        hl = sb("hl", [FM, FC, GT], F32R)
        y = sb("y", [S, 2, GB, E])

        pT = ps("pT", [P, EC, 512])
        ph = ps("ph", [P, 2, 2, 512])
        po = ps("po", [P, 2, 512])

        loaded = sig("weights_loaded", 0)
        constants = sig("constants_set", 0)
        w3_zeroed = sig("w3_zeroed", 0)
        quant = sig("quantising_steps", 0)
        totals = sig("totals_filled", 0)
        quantised = sig("weights_quantised", 0)
        x_loaded = Transfer(ctx, nc, "f_x_loaded")
        y_stored = Transfer(ctx, nc, "f_y_stored", 16)
        row_stats = sig("row_stats", GB)
        stats_complete = sig("row_stats_complete", 1)
        row_mv = sig("row_mean_var", GB)
        row_veps = sig("row_var_eps", 1)
        row_rstd = sig("row_rstd", 1)
        xn_ready = sig("xn_ready", GB)
        xn_turned = sig("xn_turned", EC, EC)
        x_high = sig("x_high_ready", EC)
        x_low = sig("x_low_ready", EC, EC)
        h_filled = sig("hidden_filled", FC, 2 * FC)
        gate_tanh = sig("gate_tanh", FC)
        gated = sig("hidden_gated", FC, 2)
        h_high = sig("hidden_high_ready", FC, 2)
        h_low = sig("hidden_low_ready", FC, 2)
        o_filled = sig("output_filled", GB)
        y_ready = sig("output_ready", GB, 2 * GB)
        block = ctx.enter_context(nc.Block())
        LOADS = 5

        @block.sync
        def _(sp):
            def load(k, parity):
                sp.wait_ge(y_ready.sem, y_ready.at(k - 2, GB))
                src = d["x2"][bass.ds(k * GB, GB)].rearrange("b s e -> s b e")
                sp.dma_start(x[:, parity], src).then_inc(x_loaded.sems[parity], 16)

            def slot(k, parity, more):
                if more:
                    load(k + 1, 1 - parity)
                sp.wait_ge(y_ready.sem, y_ready.at(k, GB))
                dst = d["out"][bass.ds(k * GB, GB)].rearrange("b s e -> s b e")
                sp.dma_start(dst, y[:, parity]).then_inc(y_stored.sems[parity], 16)

            whole = F // FM
            for parity in range(2):
                sp.sem_inc(y_stored.sems[parity], y_stored.credit)
            sp.wait_ge(w3_zeroed.sem, 1)
            for dst, src in ((w[0][:], d["w1T"].rearrange("(c p) f -> p c f", p=P)),
                             (w[1][:], d["w2T"].rearrange("(c p) f -> p c f", p=P)),
                             (w[2][0:FM, 0:whole], d["w3T"][0:whole * FM].rearrange("(c p) e -> p c e", p=FM)),
                             (w[2][0:F - whole * FM, whole], d["w3T"][whole * FM:F]),
                             (ident[:], d["ident"])):
                sp.dma_start(dst, src).then_inc(loaded.sem, 16)
            load(0, 0)
            for_groups(sp, slot)
            for parity in range(2):
                sp.wait_ge(y_stored.sems[parity], y_stored.done(NG - 2 + parity, parity))

        @block.gpsimd
        def _(pool):
            pool.memset(w[2][:], 0.0).then_inc(w3_zeroed.sem, 1)
            pool.memset(mhalf[:], -0.5).then_inc(constants.sem, 1)
            pool.memset(ones[:], 1.0).then_inc(constants.sem, 1)
            pool.wait_ge(constants.sem, 2)

            def rows_rstd(k):
                pool.wait_ge(row_veps.sem, row_veps.at(k, 1))
                pool.tensor_tensor(rstd[:], veps[:], mhalf[:], ALU.pow).then_inc(row_rstd.sem, 1)

            def slot(k, parity, more):
                if more:
                    rows_rstd(k + 1)

            rows_rstd(0)
            for_groups(pool, slot)

        @block.scalar
        def _(act):
            act.sem_inc(h_high.sem, h_high.credit)

            def copy_high(k, parity):
                act.wait_ge(h_filled.sem, h_filled.at(k - 2, FC))
                for c in range(EC):
                    act.wait_ge(xn_turned.sem, xn_turned.at(k, c + 1))
                    act.copy(xh[:, parity, c], pT[:, c, 0:GT]).then_inc(x_high.sem, 1)

            def slot(k, parity, more):
                for m in range(FC):
                    n = hidden_rows(m)
                    act.wait_ge(h_filled.sem, h_filled.at(k, m + 1))
                    act.wait_ge(gated.sem, gated.at(k, m - 1))
                    act.activation(th[0:n, m % 2], ph[0:n, m % 2, 0, 0:GT], ACT.Tanh,
                                   scale=0.5).then_inc(gate_tanh.sem, 1)
                    if m == 0:
                        act.wait_ge(o_filled.sem, o_filled.at(k, 0))
                    act.wait_ge(gated.sem, gated.at(k, m + 1))
                    act.copy(hh[0:n, m], hid[0:n, m % 2]).then_inc(h_high.sem, 1)
                if more:
                    copy_high(k + 1, 1 - parity)

            copy_high(0, 0)
            for_groups(act, slot)

        @block.vector
        def _(dve):
            dve.wait_ge(loaded.sem, 16 * LOADS)
            sizes = [EC * F, EC * F, FC * E]
            flat = [t[:].rearrange("p c n -> p (c n)") for t in w]
            steps = [0]

            def step(ins):
                steps[0] += 1
                ins.then_inc(quant.sem, 1)

            for i in range(3):
                piece = 64
                step(dve.tensor_reduce(part[:, i, 0:sizes[i] // piece], flat[i].rearrange("p (a n) -> p a n", n=piece),
                                       AX.X, ALU.add, apply_absolute_value=True))
            dve.wait_ge(quant.sem, steps[0])
            for i in range(3):
                step(dve.tensor_reduce(total[:, i:i + 1], part[:, i, 0:sizes[i] // 64], AX.X, ALU.add))
            dve.wait_ge(totals.sem, 1)
            step(dve.tensor_scalar(mean[:], po[:, 0, 0:3], 1.0 / (F * E), FW_EPS, ALU.mult, ALU.add))
            dve.wait_ge(quant.sem, steps[0])
            step(dve.tensor_scalar(thr[:], mean[:], 0.5, None, ALU.mult))
            step(dve.tensor_scalar(nthr[:], mean[:], -0.5, None, ALU.mult))
            dve.wait_ge(quant.sem, steps[0])
            for i in range(3):
                step(dve.tensor_scalar(above[:, 0:sizes[i]], flat[i], thr[:, i:i + 1], None, ALU.is_gt))
                step(dve.tensor_scalar(below[:, 0:sizes[i]], flat[i], nthr[:, i:i + 1], None, ALU.is_lt))
                dve.wait_ge(quant.sem, steps[0])
                if i < 2:
                    dve.tensor_tensor(t12[:, i].rearrange("p c f -> p (c f)"), above[:, 0:sizes[i]],
                                      below[:, 0:sizes[i]], ALU.subtract).then_inc(quantised.sem, 1)
                    dve.wait_ge(quantised.sem, i + 1)
                else:
                    step(dve.tensor_tensor(flat[2], above[:, 0:sizes[i]], below[:, 0:sizes[i]], ALU.subtract))
                    dve.wait_ge(quant.sem, steps[0])
                    dve.tensor_scalar(t3[:].rearrange("p c e -> p (c e)"), flat[2], 0.5, None,
                                      ALU.mult).then_inc(quantised.sem, 1)
            dve.sem_inc(x_low.sem, x_low.credit)
            dve.sem_inc(gated.sem, gated.credit)
            dve.sem_inc(h_low.sem, h_low.credit)
            dve.sem_inc(y_ready.sem, y_ready.credit)

            def row_statistics(k, parity):
                dve.wait_ge(x_loaded.sems[parity], x_loaded.done(k, parity))
                for b in range(GB):
                    dve.bn_stats(stats[:, b], x[:, parity, b]).then_inc(row_stats.sem, 1)
                dve.wait_ge(row_stats.sem, row_stats.at(k, GB))
                dve.sem_inc(stats_complete.sem, 1)
                for b in range(GB):
                    dve.bn_aggr(mv[:, b], stats[:, b]).then_inc(row_mv.sem, 1)
                dve.wait_ge(row_mv.sem, row_mv.at(k, GB))
                dve.tensor_scalar(veps[:], mv[:, :, 1], EPS, None, ALU.add).then_inc(row_veps.sem, 1)

            def normalise(k, parity):
                dve.wait_ge(row_rstd.sem, row_rstd.at(k, 1))
                dve.wait_ge(xn_turned.sem, xn_turned.at(k - 1, EC))
                for b in range(GB):
                    dve.tensor_scalar(xn[:, b], x[:, parity, b], mv[:, b, 0:1], rstd[:, b:b + 1],
                                      ALU.subtract, ALU.mult).then_inc(xn_ready.sem, 1)

            def split_low(k, parity):
                for c in range(EC):
                    dve.wait_ge(x_high.sem, x_high.at(k, c + 1))
                    dve.tensor_tensor(xl[:, parity, c], pT[:, c, 0:GT], xh[:, parity, c].bitcast(F32),
                                      ALU.subtract).then_inc(x_low.sem, 1)

            def gate(k, m):
                n = hidden_rows(m)
                dve.wait_ge(gate_tanh.sem, gate_tanh.at(k, m + 1))
                dve.wait_ge(h_low.sem, h_low.at(k, m - 1))
                dve.scalar_tensor_tensor(hid[0:n, m % 2], th[0:n, m % 2], 1.0, ph[0:n, m % 2, 1, 0:GT],
                                         ALU.add, ALU.mult).then_inc(gated.sem, 1)

            def low(k, m):
                n = hidden_rows(m)
                dve.wait_ge(h_high.sem, h_high.at(k, m + 1))
                dve.tensor_tensor(hl[0:n, m], hid[0:n, m % 2], hh[0:n, m].bitcast(F32),
                                  ALU.subtract).then_inc(h_low.sem, 1)

            def slot(k, parity, more):
                if more:
                    row_statistics(k + 1, 1 - parity)
                for m in range(FC):
                    gate(k, m)
                    if m >= 1:
                        low(k, m - 1)
                    if m == 1 and more:
                        normalise(k + 1, 1 - parity)
                low(k, FC - 1)
                if more:
                    split_low(k + 1, 1 - parity)
                dve.wait_ge(y_stored.sems[parity], y_stored.done(k - 2, parity))
                for b in range(GB):
                    dve.wait_ge(o_filled.sem, o_filled.at(k, b + 1))
                    dve.tensor_tensor(y[:, parity, b], po[0:S, b % 2, 0:E], x[:, parity, b],
                                      ALU.add).then_inc(y_ready.sem, 1)

            row_statistics(0, 0)
            normalise(0, 0)
            split_low(0, 0)
            for_groups(dve, slot)

        @block.tensor
        def _(pe):
            pe.sem_inc(xn_turned.sem, xn_turned.credit)
            pe.sem_inc(h_filled.sem, h_filled.credit)
            pe.wait_ge(constants.sem, 2)
            pe.wait_ge(quant.sem, 6)
            pe.matmul(po[:, 0, 0:3], ones[:], total[:], start=True, stop=True).then_inc(totals.sem, 1)

            def turn_xn(k):
                pe.wait_ge(xn_ready.sem, xn_ready.at(k, GB))
                pe.wait_ge(x_low.sem, x_low.at(k - 1, EC))
                for c in range(EC):
                    for b in range(GB):
                        mm = pe.transpose(pT[:, c, b * S:(b + 1) * S], xn[:, b, c * P:(c + 1) * P], ident[0:S, 0:S])
                    mm.then_inc(xn_turned.sem, 1)

            def hidden(k, parity, m):
                n = hidden_rows(m)
                pe.wait_ge(gated.sem, gated.at(k, m - 1))
                for i in range(2):
                    terms = [(xx, kc) for xx in (xh, xl) for kc in range(EC)]
                    for j, (xx, kc) in enumerate(terms):
                        mm = pe.matmul(ph[0:n, m % 2, i, 0:GT], t12[:, i, kc, m * FM:m * FM + n], xx[:, parity, kc],
                                       start=j == 0, stop=j == len(terms) - 1)
                mm.then_inc(h_filled.sem, 1)

            def output(k, b):
                pe.wait_ge(y_ready.sem, y_ready.at(k, b - 1))
                for m in range(FC):
                    n = hidden_rows(m)
                    for hx in (hh, hl):
                        mm = pe.matmul(po[0:S, b % 2, 0:E], hx[0:n, m, b * S:(b + 1) * S], t3[0:n, m],
                                       start=m == 0 and hx is hh, stop=m == FC - 1 and hx is hl)
                mm.then_inc(o_filled.sem, 1)

            def slot(k, parity, more):
                pe.wait_ge(x_low.sem, x_low.at(k, EC))
                for m in range(FC):
                    hidden(k, parity, m)
                if more:
                    turn_xn(k + 1)
                pe.wait_ge(h_low.sem, h_low.at(k, FC))
                for b in range(GB):
                    output(k, b)

            pe.wait_ge(loaded.sem, 16 * LOADS)
            turn_xn(0)
            pe.wait_ge(quantised.sem, 3)
            for_groups(pe, slot)


def layout_ffn(i):
    return {"w1T": np.ascontiguousarray(i["L0_ffn_w1"].T), "w2T": np.ascontiguousarray(i["L0_ffn_w2"].T),
            "w3T": np.ascontiguousarray(i["L0_ffn_w3"].T), "ident": np.eye(P, dtype=np.float32)}


def build(nc, d):
    for name, shape in (("x1", (B, S, E)), ("x2", (B, S, E)), ("qp", (B, 2, DC, QROWS)), ("m", (2, MB, MR))):
        d[name] = nc.dram_tensor("scratch_" + name, shape, F32, kind="Internal").ap()
    phase_retention(nc, d)
    phase_queries(nc, d)
    phase_cross_attention(nc, d)
    phase_ffn(nc, d)


def kernel(**inputs):
    import concourse.bacc as bacc
    from concourse.bass_utils import run_bass_kernel_spmd

    i = {name: np.asarray(a) for name, a in inputs.items()}
    arrays = {}
    for layout in (layout_retention, layout_queries, layout_cross, layout_ffn):
        arrays.update(layout(i))
    nc = bacc.Bacc("TRN2", target_bir_lowering=False, num_devices=1)
    d, given = {}, {}
    for name, a in arrays.items():
        a = np.ascontiguousarray(a)
        given["in_" + name] = a
        d[name] = nc.dram_tensor("in_" + name, a.shape, mybir.dt.from_np(a.dtype), kind="ExternalInput").ap()
    d["out"] = nc.dram_tensor("out_0", (B, S, E), F32, kind="ExternalOutput").ap()
    build(nc, d)
    result = run_bass_kernel_spmd(nc, [given], core_ids=[0])
    return result.results[0]["out_0"]
```

```python
from contextlib import ExitStack

import numpy as np

import concourse.bass as bass
from concourse import mybir

F32 = mybir.dt.float32
F32R = mybir.dt.float32r
ALU = mybir.AluOpType
ACT = mybir.ActivationFunctionType
AX = mybir.AxisListType

B, S, E = 32, 100, 256
H, HD = 16, 16
L, DC = 1444, 64
K, DQ, R = 128, 192, 64
F = 704
P = 128
EC = E // P
GB = 4
NG = B // GB
GT = GB * S
EPS = 1e-5


class Signal:

    def __init__(self, ctx, nc, name, each, credit=0):
        self.sem = ctx.enter_context(nc.semaphore(name))
        self.each, self.credit = each, credit

    def at(self, k, count):
        return k * self.each + (count + self.credit)


class Transfer:

    def __init__(self, ctx, nc, name, credit=0, amount=16):
        self.sems = [ctx.enter_context(nc.semaphore(name + str(parity))) for parity in range(2)]
        self.credit, self.amount = credit, amount

    def done(self, k, parity):
        return k * (self.amount // 2) + (self.amount - self.amount // 2 * parity + self.credit)


def wait(eng, sem, value):
    if not (isinstance(value, int) and value <= 0):
        eng.wait_ge(sem, value)


class Ahead:

    def __init__(self, ctx, nc, name):
        self.ctx, self.nc, self.name, self.loads = ctx, nc, name, []
        self.loaded = ctx.enter_context(nc.semaphore(name + "_weights_ahead"))

    def tensor(self, name, shape, src):
        t = self.ctx.enter_context(self.nc.sbuf_tensor(f"{self.name}_{name}", shape, F32, side="right"))
        self.loads.append((t, src))
        return t

    def load(self, queue):
        for t, src in self.loads:
            queue.dma_start(t[:], src).then_inc(self.loaded, 16)

    def wait(self, eng):
        eng.wait_ge(self.loaded, 16 * len(self.loads))


def for_groups(eng, slot):
    slot(0, 0, True)
    with eng.Fori(0, (NG - 2) // 2) as i:
        for parity in (1, 0):
            slot(i * 2 + (2 - parity), parity, True)
    slot(NG - 1, 1, False)


def is_first(k):
    return isinstance(k, int) and k == 0


def for_groups_ahead(sp, slot):
    slot(0, 0, True)
    with sp.Fori(0, (NG - 4) // 2) as i:
        for parity in (1, 0):
            slot(i * 2 + (2 - parity), parity, True)
    slot(NG - 3, 1, True)
    for k in range(NG - 2, NG):
        slot(k, k % 2, False)


def phase_retention(nc, d, ahead):
    with ExitStack() as ctx:
        def sb(name, shape, dt=F32):
            return ctx.enter_context(nc.sbuf_tensor("a_" + name, shape, dt))

        def ps(name, shape):
            return ctx.enter_context(nc.psum_tensor("a_" + name, shape, F32))

        def sig(name, each, credit=0):
            return Signal(ctx, nc, "a_" + name, each, credit)

        wqk = sb("wqk", [P, 2, EC, E])
        wvg = sb("wvg", [P, EC, 2 * E])
        wqkh = sb("wqkh", [P, 2, EC, E], F32R)
        wvgh = sb("wvgh", [P, EC, 2 * E], F32R)
        wqkl = sb("wqkl", [P, 2, EC, E], F32R)
        wvgl = sb("wvgl", [P, EC, 2 * E], F32R)
        wo = sb("wo", [P, EC, E])
        bqk = sb("bqk", [P, 2, EC])
        bvg = sb("bvg", [S, 2 * E])
        gnw = sb("gnw", [S, E])
        gnb = sb("gnb", [S, E])
        bo = sb("bo", [S, E])
        decay = sb("decay", [S, H])
        rel = sb("rel", [S, S])
        causal = sb("causal", [S, S])
        headmask = sb("headmask", [P, 8])
        ident = sb("ident", [P, P])
        dmask = sb("dmask", [S, H, S])
        mhalf = sb("mhalf", [S, GB * H])
        x = sb("x", [S, 2, GB, E])
        stats = sb("stats", [S, GB, 6])
        mv = sb("mv", [S, GB, 2])
        veps = sb("veps", [S, GB])
        rstd = sb("rstd", [S, GB])
        xn = sb("xn", [S, GB, E])
        xh = sb("xh", [P, EC, GT], F32R)
        xl = sb("xl", [P, EC, GT], F32R)
        kT = sb("kT", [P, EC, GT])
        vaug = sb("vaug", [S, 2, GB, H, 2 * HD])
        z = sb("z", [S, 2, GB, E])
        qT = sb("qT", [P, EC, GT])
        qm = sb("qm", [P, EC, 8, GT])
        ret = sb("ret", [S, 2, H, S])
        av = sb("av", [P, GT])
        neg = sb("neg", [S, GB, H])
        den = sb("den", [S, GB, H])
        rec = sb("rec", [S, GB, H])
        att = sb("att", [S, GB * H, HD])
        s1 = sb("s1", [S, GB * H])
        mean = sb("mean", [S, GB * H])
        cent = sb("cent", [S, GB * H, HD])
        s2 = sb("s2", [S, GB * H])
        gveps = sb("gveps", [S, GB * H])
        grstd = sb("grstd", [S, GB * H])
        gn = sb("gn", [S, GB, E])
        gate = sb("gate", [S, GB, E])
        gatew = sb("gatew", [S, GB, E])
        gateb = sb("gateb", [S, GB, E])
        y = sb("y", [S, GB, E])
        yT = sb("yT", [P, EC, GT])
        x1 = sb("x1", [S, 2, GB, E])

        ring = ps("ring", [P, 2, 512])
        sc = ps("sc", [P, 2, 512])
        pav = ps("pav", [P, 512])
        pt = ps("pt", [P, 512])
        po = ps("po", [P, 2, 512])

        weights_loaded = sig("weights_loaded", 0)
        later_loaded = sig("later_weights_loaded", 0)
        decay_exp = sig("decay_exponentials", 0)
        mask_ready = sig("decay_mask_ready", 0)
        constants = sig("constants_set", 0)
        gn_halved = sig("gn_halved", 0)
        x_loaded = Transfer(ctx, nc, "a_x_loaded")
        row_stats = sig("row_stats", GB)
        stats_complete = sig("row_stats_complete", 1)
        row_mv = sig("row_mean_var", GB)
        row_veps = sig("row_var_eps", 1)
        row_rstd = sig("row_rstd", 1)
        xn_ready = sig("xn_ready", GB, GB)
        x_low = sig("x_low_ready", EC)
        w_high = sig("weights_high_ready", 0)
        w_low = sig("weights_low_ready", 0)
        unit = sig("ring_unit_filled", 10, 10)
        act_read = sig("ring_unit_read_by_act", 6, 6)
        dve_read = sig("ring_unit_read_by_dve", 8, 8)
        q_spread0 = sig("q_spread_lower", 1)
        q_spread1 = sig("q_spread_upper", 1)
        sc_filled = sig("scores_filled", 16, 32)
        sc_masked = sig("scores_masked", 16, 16)
        av_filled = sig("attn_filled", GB, 8)
        av_copied = sig("attn_copied", GB, 1)
        av_turned = sig("attn_turned", GB, 1)
        sums_negated = sig("row_sums_negated", GB)
        sums_clipped = sig("row_sums_clipped", GB)
        sums_inverted = sig("row_sums_inverted", GB)
        att_scaled = sig("attn_scaled", GB, 1)
        gn_sum = sig("gn_sum", 1)
        gn_mean = sig("gn_mean", 1)
        gn_centred = sig("gn_centred", 1)
        gn_squared = sig("gn_squared", 1)
        gn_sqsum = sig("gn_square_sum", 1)
        gn_veps = sig("gn_var_eps", 1)
        gn_rstd = sig("gn_rstd", 1)
        gn_scaled = sig("gn_scaled", 1)
        gn_weighted = sig("gn_weighted", 1)
        gate_tanh = sig("gate_tanh", 1)
        gate_ready = sig("gate_ready", 1, 1)
        gate_weighed = sig("gate_weighed", 2, 2)
        y_ready = sig("y_ready", 1, 1)
        y_turned = sig("y_turned", EC, 1)
        yT_copied = sig("yT_copied", EC)
        o_filled = sig("o_filled", GB, 1)
        res_biased = sig("residual_biased", 1, 2)
        x1_ready = sig("x1_ready", GB, 2 * GB)
        x1_stored = Transfer(ctx, nc, "a_x1_stored", 16)

        weights = (
            (ident[:], d["ident"]), (bqk[:, 0], d["bq"]), (bqk[:, 1], d["bk"]), (headmask[:], d["headmask"]),
            (decay[:], d["decay"]), (rel[:], d["rel"]), (causal[:], d["causal"]),
            (wqk[:, 0], d["Wq"].rearrange("(c p) n -> p c n", p=P)),
            (wqk[:, 1], d["Wk"].rearrange("(c p) n -> p c n", p=P)),
        )
        later_weights = (
            (bvg[:, 0:E], d["bv"]), (bvg[:, E:2 * E], d["bg"]),
            (wvg[:, :, 0:E], d["Wv"].rearrange("(c p) n -> p c n", p=P)),
            (wvg[:, :, E:2 * E], d["Wg"].rearrange("(c p) n -> p c n", p=P)),
            (bo[:], d["bo"]), (gnw[:], d["gn_w"]), (gnb[:], d["gn_b"]),
            (wo[:], d["Wo"].rearrange("(c p) n -> p c n", p=P)),
        )
        W_ALL, LATER_ALL = 16 * len(weights), 16 * len(later_weights)
        block = ctx.enter_context(nc.Block())

        @block.sync
        def _(sp):
            def load(k, parity):
                sp.wait_ge(res_biased.sem, res_biased.at(k - 2, 1))
                src = d["x"][bass.ds(k * GB, GB)].rearrange("b s e -> s b e")
                sp.dma_start(x[:, parity], src).then_inc(x_loaded.sems[parity], 16)

            def store(k, parity):
                sp.wait_ge(x1_ready.sem, x1_ready.at(k, GB))
                dst = d["x1"][bass.ds(k * GB, GB)].rearrange("b s e -> s b e")
                sp.dma_start(dst, x1[:, parity]).then_inc(x1_stored.sems[parity], 16)

            def slot(k, parity, more):
                if more:
                    load(k + 2, parity)
                if not is_first(k):
                    store(k - 1, 1 - parity)

            for parity in range(2):
                sp.sem_inc(x1_stored.sems[parity], x1_stored.credit)
            load(0, 0)
            for dst, src in weights:
                sp.dma_start(dst, src).then_inc(weights_loaded.sem, 16)
            for dst, src in later_weights:
                sp.dma_start(dst, src).then_inc(later_loaded.sem, 16)
            load(1, 1)
            for weights_ahead in ahead:
                weights_ahead.load(sp)
            for_groups_ahead(sp, slot)
            store(NG - 1, 1)
            for parity in range(2):
                sp.wait_ge(x1_stored.sems[parity], x1_stored.done(NG - 2 + parity, parity))

        @block.gpsimd
        def _(pool):
            def rows_rstd(k):
                pool.wait_ge(row_veps.sem, row_veps.at(k, 1))
                pool.tensor_tensor(rstd[:], veps[:], mhalf[:, 0:GB], ALU.pow).then_inc(row_rstd.sem, 1)

            for s in (res_biased, gate_weighed):
                pool.sem_inc(s.sem, s.credit)
            pool.memset(mhalf[:], -0.5).then_inc(constants.sem, 1)
            pool.memset(vaug[:], 1.0).then_inc(constants.sem, 1)
            pool.wait_ge(constants.sem, 2)
            rows_rstd(0)
            pool.wait_ge(later_loaded.sem, LATER_ALL)
            pool.tensor_scalar(gnw[:], gnw[:], 0.5, 1.0, ALU.mult, ALU.mult).then_inc(gn_halved.sem, 1)
            pool.tensor_scalar(gnb[:], gnb[:], 0.5, 1.0, ALU.mult, ALU.mult).then_inc(gn_halved.sem, 1)
            pool.wait_ge(gn_halved.sem, 2)

            def group_rstd(k):
                pool.wait_ge(gn_veps.sem, gn_veps.at(k, 1))
                pool.tensor_tensor(grstd[:], gveps[:], mhalf[:], ALU.pow).then_inc(gn_rstd.sem, 1)

            def weigh_gate(k):
                pool.wait_ge(y_ready.sem, y_ready.at(k, 0))
                pool.wait_ge(gate_ready.sem, gate_ready.at(k, 1))
                for out, t in ((gatew, gnw), (gateb, gnb)):
                    pool.tensor_tensor(out[:], gate[:], t[:].unsqueeze(1).broadcast_to([S, GB, E]),
                                       ALU.mult).then_inc(gate_weighed.sem, 1)

            def slot(k, parity, more):
                if more:
                    rows_rstd(k + 1)
                if not is_first(k):
                    group_rstd(k - 1)
                pool.wait_ge(xn_ready.sem, xn_ready.at(k, GB))
                pool.wait_ge(x_loaded.sems[parity], x_loaded.done(k, parity))
                pool.wait_ge(x1_stored.sems[parity], x1_stored.done(k - 2, parity))
                pool.tensor_tensor(x1[:, parity], x[:, parity], bo[:].unsqueeze(1).broadcast_to([S, GB, E]),
                                   ALU.add).then_inc(res_biased.sem, 1)
                weigh_gate(k)

            for_groups(pool, slot)
            group_rstd(NG - 1)

        @block.scalar
        def _(act):
            act.wait_ge(weights_loaded.sem, W_ALL)
            for s in (act_read, av_copied):
                act.sem_inc(s.sem, s.credit)
            for h in range(H):
                act.activation(dmask[:, h], rel[:], ACT.Exp, scale=decay[:, h:h + 1]).then_inc(decay_exp.sem, 1)

            def copy_xnT(k):
                act.wait_ge(unit.sem, unit.at(k - 1, 10))
                for c in range(EC):
                    act.wait_ge(unit.sem, unit.at(k, c + 1))
                    act.copy(xh[:, c], ring[:, c, 0:GT]).then_inc(act_read.sem, 1)

            def copy_qk(k, w):
                if w == 0:
                    wait(act, q_spread1.sem, q_spread1.at(k - 1, 1))
                else:
                    act.wait_ge(sc_filled.sem, sc_filled.at(k - 1, 16))
                for c, (dst, u) in enumerate(((qT, 2), (qT, 3)) if w == 0 else ((kT, 4), (kT, 5))):
                    act.wait_ge(unit.sem, unit.at(k, u + 1))
                    act.activation(dst[:, c], ring[:, c, 0:GT], ACT.Identity,
                                   bias=bqk[:, w, c:c + 1]).then_inc(act_read.sem, 1)

            def spread_lower(k):
                act.wait_ge(act_read.sem, act_read.at(k, 4))
                for h in range(8):
                    cp = act.activation(qm[:, 0, h], qT[:, 0], ACT.Copy, scale=headmask[:, h:h + 1])
                cp.then_inc(q_spread0.sem, 1)

            def copy_attn(k, b):
                act.wait_ge(av_filled.sem, av_filled.at(k, b + 1))
                act.wait_ge(av_turned.sem, av_turned.at(k, b))
                act.copy(av[:], pav[:, 0:GT]).then_inc(av_copied.sem, 1)

            def copy_y(k):
                act.wait_ge(o_filled.sem, o_filled.at(k, 0))
                for c in range(EC):
                    act.wait_ge(y_turned.sem, y_turned.at(k, c + 1))
                    act.copy(yT[:, c], po[:, c, 0:GT]).then_inc(yT_copied.sem, 1)

            def slot(k, parity, more):
                act.wait_ge(dve_read.sem, dve_read.at(k, 8))
                act.wait_ge(gate_weighed.sem, gate_weighed.at(k, 0))
                act.activation(gate[:], z[:, parity], ACT.Tanh, scale=0.5).then_inc(gate_tanh.sem, 1)
                for b in range(2):
                    copy_attn(k, b)
                if more:
                    copy_xnT(k + 1)
                copy_attn(k, 2)
                if more:
                    copy_qk(k + 1, 0)
                copy_attn(k, 3)
                if more:
                    copy_qk(k + 1, 1)
                if not is_first(k):
                    copy_y(k - 1)
                if more:
                    spread_lower(k + 1)
                act.wait_ge(gn_centred.sem, gn_centred.at(k, 1))
                act.activation(gn[:].rearrange("p b (h e) -> p (b h) e", h=H), cent[:],
                               ACT.Square).then_inc(gn_squared.sem, 1)

            copy_xnT(0)
            for w in range(2):
                copy_qk(0, w)
            spread_lower(0)
            for_groups(act, slot)
            copy_y(NG - 1)

        @block.vector
        def _(dve):
            for s in (xn_ready, dve_read, sc_masked, x1_ready, gate_ready, att_scaled, y_ready):
                dve.sem_inc(s.sem, s.credit)

            def row_sums(k, parity, half):
                dve.wait_ge(x_loaded.sems[parity], x_loaded.done(k, parity))
                for b in half:
                    dve.bn_stats(stats[:, b], x[:, parity, b]).then_inc(row_stats.sem, 1)

            def row_variances(k):
                dve.wait_ge(row_stats.sem, row_stats.at(k, GB))
                dve.sem_inc(stats_complete.sem, 1)
                for b in range(GB):
                    dve.bn_aggr(mv[:, b], stats[:, b]).then_inc(row_mv.sem, 1)
                dve.wait_ge(row_mv.sem, row_mv.at(k, GB))
                dve.tensor_scalar(veps[:], mv[:, :, 1], EPS, None, ALU.add).then_inc(row_veps.sem, 1)

            def normalise(k, parity, half):
                dve.wait_ge(row_rstd.sem, row_rstd.at(k, 1))
                dve.wait_ge(unit.sem, unit.at(k - 1, 2))
                for b in half:
                    dve.tensor_scalar(xn[:, b], x[:, parity, b], mv[:, b, 0:1], rstd[:, b:b + 1],
                                      ALU.subtract, ALU.mult).then_inc(xn_ready.sem, 1)

            def split_low(k):
                dve.wait_ge(unit.sem, unit.at(k - 1, 10))
                for c in range(EC):
                    dve.wait_ge(act_read.sem, act_read.at(k, c + 1))
                    dve.tensor_tensor(xl[:, c], ring[:, c, 0:GT], xh[:, c].bitcast(F32),
                                      ALU.subtract).then_inc(x_low.sem, 1)

            def split_weights(w, high, low, n):
                dve.tensor_copy(high[:], w[:]).then_inc(w_high.sem, 1)
                dve.wait_ge(w_high.sem, n)
                dve.tensor_tensor(low[:], w[:], high[:].bitcast(F32), ALU.subtract).then_inc(w_low.sem, 1)

            def read_vg(k, parity, b):
                u = 6 + b
                dve.wait_ge(unit.sem, unit.at(k, u + 1))
                dve.tensor_tensor(vaug[:, parity, b, :, 0:HD],
                                  ring[0:S, u % 2, 0:E].rearrange("p (h e) -> p h e", h=H),
                                  bvg[:, 0:E].rearrange("p (h e) -> p h e", h=H),
                                  ALU.add).then_inc(dve_read.sem, 1)
                dve.tensor_tensor(z[:, parity, b], ring[0:S, u % 2, E:2 * E], bvg[:, E:2 * E],
                                  ALU.add).then_inc(dve_read.sem, 1)

            def mask_scores(k, b, between={}):
                dve.wait_ge(av_filled.sem, av_filled.at(k, b - 1))
                for j in range(4):
                    dve.wait_ge(sc_filled.sem, sc_filled.at(k, 4 * b + j + 1))
                    dve.tensor_tensor(ret[:, b % 2, 4 * j:4 * j + 4],
                                      sc[0:S, j % 2, 0:GT].rearrange("p (h s) -> p h s", h=4),
                                      dmask[:, 4 * j:4 * j + 4], ALU.mult).then_inc(sc_masked.sem, 1)
                    if j in between:
                        between[j]()

            turned = pt[0:S, :].rearrange("p (h e) -> p h e", h=H)

            def scale_attn(k, b):
                dve.wait_ge(av_turned.sem, av_turned.at(k, b + 1))
                dve.tensor_scalar(neg[:, b], turned[:, :, HD], -1.0, 1.0, ALU.mult,
                                  ALU.max).then_inc(sums_negated.sem, 1)
                dve.wait_ge(sums_negated.sem, sums_negated.at(k, b + 1))
                dve.scalar_tensor_tensor(den[:, b], turned[:, :, HD], 1.0, neg[:, b], ALU.max,
                                         ALU.max).then_inc(sums_clipped.sem, 1)
                dve.wait_ge(sums_clipped.sem, sums_clipped.at(k, b + 1))
                dve.reciprocal(rec[:, b], den[:, b]).then_inc(sums_inverted.sem, 1)
                dve.wait_ge(sums_inverted.sem, sums_inverted.at(k, b + 1))
                dve.tensor_tensor(att[:, b * H:(b + 1) * H], turned[:, :, 0:HD],
                                  rec[:, b].unsqueeze(2).broadcast_to([S, H, HD]),
                                  ALU.mult).then_inc(att_scaled.sem, 1)

            def wide(t):
                return t[:].unsqueeze(2).broadcast_to([S, GB * H, HD])

            def spread_upper(k):
                dve.wait_ge(act_read.sem, act_read.at(k, 4))
                dve.wait_ge(sc_filled.sem, sc_filled.at(k - 1, 16))
                for h in range(8):
                    cp = dve.tensor_scalar(qm[:, 1, h], qT[:, 1], headmask[:, h:h + 1], None, ALU.mult)
                cp.then_inc(q_spread1.sem, 1)

            def sum_heads(k):
                dve.wait_ge(att_scaled.sem, att_scaled.at(k, GB))
                dve.tensor_reduce(s1[:], att[:], AX.X, ALU.add).then_inc(gn_sum.sem, 1)

            def centre(k):
                dve.wait_ge(gn_sum.sem, gn_sum.at(k, 1))
                dve.tensor_scalar(mean[:], s1[:], 1.0 / HD, None, ALU.mult).then_inc(gn_mean.sem, 1)
                dve.wait_ge(gn_mean.sem, gn_mean.at(k, 1))
                dve.tensor_tensor(cent[:], att[:], wide(mean), ALU.subtract).then_inc(gn_centred.sem, 1)

            def variance(k):
                dve.wait_ge(gn_squared.sem, gn_squared.at(k, 1))
                dve.tensor_reduce(s2[:], gn[:].rearrange("p b (h e) -> p (b h) e", h=H), AX.X,
                                  ALU.add).then_inc(gn_sqsum.sem, 1)
                dve.wait_ge(gn_sqsum.sem, gn_sqsum.at(k, 1))
                dve.tensor_scalar(gveps[:], s2[:], 1.0 / HD, EPS, ALU.mult, ALU.add).then_inc(gn_veps.sem, 1)

            def scale_norm(k):
                dve.wait_ge(gn_rstd.sem, gn_rstd.at(k, 1))
                dve.tensor_tensor(gn[:].rearrange("p b (h e) -> p (b h) e", h=H), cent[:], wide(grstd),
                                  ALU.mult).then_inc(gn_scaled.sem, 1)

            def apply_gate(k):
                dve.wait_ge(gate_weighed.sem, gate_weighed.at(k, 2))
                dve.wait_ge(gn_scaled.sem, gn_scaled.at(k, 1))
                dve.tensor_tensor(gn[:], gn[:], gatew[:], ALU.mult).then_inc(gn_weighted.sem, 1)
                dve.wait_ge(gn_weighted.sem, gn_weighted.at(k, 1))
                dve.wait_ge(y_turned.sem, y_turned.at(k, 0))
                dve.tensor_tensor(y[:], gn[:], gateb[:], ALU.add).then_inc(y_ready.sem, 1)

            def make_gate(k, parity):
                dve.wait_ge(gate_tanh.sem, gate_tanh.at(k, 1))
                dve.wait_ge(gate_weighed.sem, gate_weighed.at(k, 0))
                dve.scalar_tensor_tensor(gate[:], gate[:], 1.0, z[:, parity], ALU.add,
                                         ALU.mult).then_inc(gate_ready.sem, 1)

            def add_output(k, parity, b):
                if b == 0:
                    dve.wait_ge(res_biased.sem, res_biased.at(k, 1))
                dve.wait_ge(o_filled.sem, o_filled.at(k, b + 1))
                dve.tensor_tensor(x1[:, parity, b], po[0:S, b % 2, 0:E], x1[:, parity, b],
                                  ALU.add).then_inc(x1_ready.sem, 1)

            def slot(k, parity, more):
                before = not is_first(k)
                mask_scores(k, 0)
                mask_scores(k, 1, {0: lambda: row_sums(k + 1, 1 - parity, (0, 1)),
                                   1: lambda: row_sums(k + 1, 1 - parity, (2, 3)),
                                   2: lambda: row_variances(k + 1)} if more else {})
                mask_scores(k, 2, {0: lambda: normalise(k + 1, 1 - parity, (0, 1)),
                                   1: lambda: normalise(k + 1, 1 - parity, (2, 3)),
                                   2: lambda: scale_attn(k, 0)} if more else {2: lambda: scale_attn(k, 0)})
                mask_scores(k, 3, {1: lambda: split_low(k + 1) if more else None, 2: lambda: scale_attn(k, 1)})
                if before:
                    scale_norm(k - 1)
                scale_attn(k, 2)
                if before:
                    apply_gate(k - 1)
                make_gate(k, parity)
                scale_attn(k, 3)
                if more:
                    dve.wait_ge(av_filled.sem, av_filled.at(k - 1, GB))
                    read_vg(k + 1, 1 - parity, 0)
                sum_heads(k)
                if more:
                    read_vg(k + 1, 1 - parity, 1)
                centre(k)
                for b in range(GB):
                    if before:
                        add_output(k - 1, 1 - parity, b)
                    if more and b < 2:
                        read_vg(k + 1, 1 - parity, 2 + b)
                    if b == 0 and more:
                        spread_upper(k + 1)
                    if b == 2:
                        variance(k)

            row_sums(0, 0, range(GB))
            row_variances(0)
            normalise(0, 0, range(GB))
            dve.wait_ge(weights_loaded.sem, W_ALL)
            split_weights(wqk, wqkh, wqkl, 1)
            split_low(0)
            dve.wait_ge(decay_exp.sem, H)
            dve.tensor_tensor(dmask[:], dmask[:], causal[:].unsqueeze(1).broadcast_to([S, H, S]),
                              ALU.mult).then_inc(mask_ready.sem, 1)
            dve.wait_ge(mask_ready.sem, 1)
            dve.wait_ge(constants.sem, 2)
            dve.wait_ge(later_loaded.sem, LATER_ALL)
            split_weights(wvg, wvgh, wvgl, 2)
            for b in range(GB):
                read_vg(0, 0, b)
            spread_upper(0)
            for_groups(dve, slot)
            scale_norm(NG - 1)
            apply_gate(NG - 1)
            for b in range(GB):
                add_output(NG - 1, 1, b)

        @block.tensor
        def _(pe):
            pe.wait_ge(weights_loaded.sem, W_ALL)
            for s in (unit, sc_filled, av_filled, av_turned, y_turned, o_filled):
                pe.sem_inc(s.sem, s.credit)

            def ring_free(k, u):
                if u < 2:
                    pe.wait_ge(dve_read.sem, dve_read.at(k - 1, 6 + 2 * u))
                elif u < 8:
                    pe.wait_ge(act_read.sem, act_read.at(k, u - 1))
                else:
                    pe.wait_ge(dve_read.sem, dve_read.at(k, 2 * (u - 8) + 2))

            def turn_xn(k):
                for c in range(EC):
                    ring_free(k, c)
                    pe.wait_ge(xn_ready.sem, xn_ready.at(k, GB))
                    for b in range(GB):
                        mm = pe.transpose(ring[:, c, b * S:(b + 1) * S], xn[:, b, c * P:(c + 1) * P],
                                          ident[0:S, 0:S])
                    mm.then_inc(unit.sem, 1)

            def terms(high, low):
                return [(w, xx, kc) for w, xx in ((high, xh), (high, xl), (low, xh)) for kc in range(EC)]

            def project_qk(k, w):
                if w == 0:
                    pe.wait_ge(x_low.sem, x_low.at(k, EC))
                for c in range(EC):
                    u = 2 + 2 * w + c
                    ring_free(k, u)
                    parts = terms(wqkh, wqkl)
                    for n, (ww, xx, kc) in enumerate(parts):
                        mm = pe.matmul(ring[:, u % 2, 0:GT], ww[:, w, kc, c * P:(c + 1) * P], xx[:, kc],
                                       start=n == 0, stop=n == len(parts) - 1)
                    mm.then_inc(unit.sem, 1)

            def project_vg(k, b):
                u = 6 + b
                ring_free(k, u)
                parts = terms(wvgh, wvgl)
                for n, (ww, xx, kc) in enumerate(parts):
                    mm = pe.matmul(ring[0:S, u % 2, :], xx[:, kc, b * S:(b + 1) * S], ww[:, kc],
                                   start=n == 0, stop=n == len(parts) - 1)
                mm.then_inc(unit.sem, 1)

            def scores(k, b, j):
                c = j // 2
                pe.wait_ge(sc_masked.sem, sc_masked.at(k, 4 * b + j - 1))
                pe.matmul(sc[0:S, j % 2, 0:GT], kT[:, c, b * S:(b + 1) * S],
                          qm[:, c, 4 * (j % 2):4 * (j % 2) + 4, b * S:(b + 1) * S],
                          start=True, stop=True).then_inc(sc_filled.sem, 1)

            def attend(k, parity, b, q):
                pe.wait_ge(sc_masked.sem, sc_masked.at(k, 4 * b + q + 1))
                if q == 0:
                    pe.wait_ge(av_copied.sem, av_copied.at(k, b))
                for g in range(4):
                    mm = pe.matmul(pav[32 * g:32 * g + 32, q * S:(q + 1) * S], vaug[:, parity, b, 4 * q + g],
                                   ret[:, b % 2, 4 * q + g], start=True, stop=True)
                if q == 3:
                    mm.then_inc(av_filled.sem, 1)

            def turn_attn(k, b):
                pe.wait_ge(av_copied.sem, av_copied.at(k, b + 1))
                pe.wait_ge(att_scaled.sem, att_scaled.at(k, b))
                for q in range(4):
                    mm = pe.transpose(pt[0:S, q * P:(q + 1) * P], av[:, q * S:(q + 1) * S], ident[:])
                mm.then_inc(av_turned.sem, 1)

            def turn_y(k):
                pe.wait_ge(y_ready.sem, y_ready.at(k, 1))
                pe.wait_ge(x1_ready.sem, x1_ready.at(k - 1, GB))
                for c in range(EC):
                    for b in range(GB):
                        mm = pe.transpose(po[:, c, b * S:(b + 1) * S], y[:, b, c * P:(c + 1) * P], ident[0:S, 0:S])
                    mm.then_inc(y_turned.sem, 1)

            def project_out(k, b):
                if b == 0:
                    pe.wait_ge(yT_copied.sem, yT_copied.at(k, EC))
                pe.wait_ge(x1_ready.sem, x1_ready.at(k, b - 1))
                for kc in range(EC):
                    mm = pe.matmul(po[0:S, b % 2, 0:E], yT[:, kc, b * S:(b + 1) * S], wo[:, kc],
                                   start=kc == 0, stop=kc == EC - 1)
                mm.then_inc(o_filled.sem, 1)

            def slot(k, parity, more):
                before = not is_first(k)
                pe.wait_ge(act_read.sem, act_read.at(k, 6))
                pe.wait_ge(q_spread0.sem, q_spread0.at(k, 1))
                pe.wait_ge(q_spread1.sem, q_spread1.at(k, 1))
                pe.wait_ge(dve_read.sem, dve_read.at(k, 8))
                for b in range(GB):
                    for j in range(4):
                        scores(k, b, j)
                        if j == 0 and b >= 2:
                            turn_attn(k, b - 2)
                        if b >= 1:
                            attend(k, parity, b - 1, j)
                    if b == 2 and more:
                        turn_xn(k + 1)
                if more:
                    project_qk(k + 1, 0)
                turn_attn(k, 2)
                for q in range(4):
                    attend(k, parity, 3, q)
                if more:
                    project_qk(k + 1, 1)
                turn_attn(k, 3)
                for b in range(GB + 2):
                    if more and b < GB:
                        project_vg(k + 1, b)
                    if before and b == 0:
                        turn_y(k - 1)
                    if before and b >= 2:
                        project_out(k - 1, b - 2)

            turn_xn(0)
            pe.wait_ge(w_low.sem, 1)
            for w in range(2):
                project_qk(0, w)
            pe.wait_ge(w_low.sem, 2)
            for b in range(GB):
                project_vg(0, b)
            for_groups(pe, slot)
            turn_y(NG - 1)
            for b in range(GB):
                project_out(NG - 1, b)


def replicate(a, rows):
    return np.ascontiguousarray(np.broadcast_to(a, (rows,) + a.shape))


def layout_retention(i):
    j = np.arange(S)
    rel = j[None, :] - j[:, None]
    p = np.arange(P)
    return {
        "x": i["x"], "Wq": i["L0_attn_Wq"], "Wk": i["L0_attn_Wk"], "Wv": i["L0_attn_Wv"], "Wg": i["L0_attn_Wg"],
        "Wo": i["L0_attn_Wo"],
        "bq": np.ascontiguousarray(i["L0_attn_bq"].reshape(EC, P).T),
        "bk": np.ascontiguousarray(i["L0_attn_bk"].reshape(EC, P).T),
        "bv": replicate(i["L0_attn_bv"], S), "bg": replicate(i["L0_attn_bg"], S),
        "gn_w": replicate(i["L0_attn_gn_w"], S), "gn_b": replicate(i["L0_attn_gn_b"], S),
        "bo": replicate(i["L0_attn_bo"], S), "decay": replicate(i["L0_attn_decay"], S),
        "rel": np.maximum(rel, 0).astype(np.float32), "causal": (rel >= 0).astype(np.float32),
        "headmask": np.where(p[:, None] // HD == np.arange(8)[None, :], HD ** -0.5, 0).astype(np.float32),
        "ident": np.eye(P, dtype=np.float32),
    }


def rope_tables(length, dim):
    inv = np.float32(1.0) / np.float32(10000.0) ** (np.arange(0, dim, 2, dtype=np.float32) / np.float32(dim))
    f = np.arange(length, dtype=np.float32)[:, None] * inv[None, :]
    return np.repeat(np.sin(f), 2, axis=-1), np.repeat(np.cos(f), 2, axis=-1)


HP = H // 2
MC = H * DQ // P


def weights_for_queries(ctx, nc, d):
    ahead = Ahead(ctx, nc, "w")
    ahead.wq = ahead.tensor("wq", [K, H, E], d["xWq"].rearrange("(h k) e -> k h e", k=K))
    ahead.wkcq = ahead.tensor("wkcq", [K, H, DQ], d["w_kc_q"].rearrange("h k q -> k h q"))
    return ahead


def phase_query_weights(nc, d, ahead, t):
    with ExitStack() as ctx:
        def sb(name, shape, dt=F32):
            return ctx.enter_context(nc.sbuf_tensor("w_" + name, shape, dt))

        def sem(name):
            return ctx.enter_context(nc.semaphore("w_" + name))

        wq, wkcq = ahead.wq, ahead.wkcq
        wqr = sb("wqr", [2 * R, HP, 3, P])
        wkr = sb("wkr", [2 * R, HP, 2 * DC])
        bank = ctx.enter_context(nc.psum_tensor("w_bank", [P, 8, 512], F32))
        loaded, filled, copied = sem("loaded"), sem("filled"), sem("copied")
        split = sem("split")
        block = ctx.enter_context(nc.Block())
        N_WC = H * EC

        @block.sync
        def _(sp):
            for dst, src in ((wqr[:], d["W_qrT"]), (wkr[:], d["W_krT"]),
                             (t["cosq"][:], d["cosq"]), (t["sinq"][:], d["sinq"])):
                sp.dma_start(dst, src).then_inc(loaded, 16)
            sp.wait_ge(loaded, 16 * 4)

        @block.tensor
        def _(pe):
            ahead.wait(pe)
            for n in range(N_WC + HP):
                if n >= 8:
                    pe.wait_ge(copied, n - 7)
                if n < N_WC:
                    h, c = n // EC, n % EC
                    pe.matmul(bank[:, n % 8, 0:DQ], wq[:, h, c * P:(c + 1) * P], wkcq[:, h],
                              start=True, stop=True).then_inc(filled, 1)
                else:
                    if n == N_WC:
                        pe.wait_ge(loaded, 16 * 4)
                    h = n - N_WC
                    for j in range(3):
                        mm = pe.matmul(bank[:, n % 8, j * P:(j + 1) * P], wqr[:, h, j], wkr[:, h],
                                       start=True, stop=True)
                    mm.then_inc(filled, 1)

        @block.scalar
        def _(act):
            for n in range(N_WC):
                h, c = n // EC, n % EC
                act.wait_ge(filled, n + 1)
                act.copy(t["wch"][:, c, h * DQ:(h + 1) * DQ], bank[:, n % 8, 0:DQ]).then_inc(split, 1)

        @block.vector
        def _(dve):
            for n in range(N_WC + HP):
                h, c = n // EC, n % EC
                dve.wait_ge(filled, n + 1)
                if n < N_WC:
                    dve.wait_ge(split, n + 1)
                    cols = slice(h * DQ, (h + 1) * DQ)
                    dve.tensor_tensor(t["wcl"][:, c, cols], bank[:, n % 8, 0:DQ], t["wch"][:, c, cols].bitcast(F32),
                                      ALU.subtract).then_inc(copied, 1)
                else:
                    pair = bank[:, n % 8, 0:3 * P].rearrange("p (j s e) -> p s j e", j=3, s=2)
                    for side in range(2):
                        cp = dve.tensor_copy(t["ac"][:, n - N_WC + side * HP], pair[:, side])
                    cp.then_inc(copied, 1)


def query_weights(ctx, nc):
    return {n: ctx.enter_context(nc.sbuf_tensor("q_" + n, shape, dt)) for n, shape, dt in (
        ("wch", [P, EC, H * DQ], F32R), ("wcl", [P, EC, H * DQ], F32R), ("ac", [P, H, 3, DC], F32),
        ("cosq", [P, 3, S], F32), ("sinq", [P, 3, S], F32))}


def phase_queries(nc, d, t, ahead):
    wch, wcl, ac, cosq, sinq = (t[n] for n in ("wch", "wcl", "ac", "cosq", "sinq"))
    with ExitStack() as ctx:
        def sb(name, shape, dt=F32):
            return ctx.enter_context(nc.sbuf_tensor("q_" + name, shape, dt))

        def ps(name, shape):
            return ctx.enter_context(nc.psum_tensor("q_" + name, shape, F32))

        def sig(name, each, credit=0):
            return Signal(ctx, nc, "q_" + name, each, credit)

        ident = sb("ident", [P, P])
        mhalf = sb("mhalf", [S, GB])
        x = sb("x", [S, 2, GB, E])
        stats = sb("stats", [S, GB, 6])
        mv = sb("mv", [S, GB, 2])
        veps = sb("veps", [S, GB])
        rstd = sb("rstd", [S, GB])
        xn = sb("xn", [S, GB, E])
        xh = sb("xh", [P, 2, EC, GT], F32R)
        xl = sb("xl", [P, 2, EC, GT], F32R)
        rot = sb("rot", [P, 2, 6, GT])
        qs = sb("qs", [DC, 2, GB, 4, S])

        pT = ps("pT", [P, EC, 512])
        pq = ps("pq", [P, 4, 512])
        pp = ps("pp", [P, 2, 512])

        ident_loaded = sig("ident_loaded", 0)
        constants = sig("constants_set", 0)
        x_loaded = Transfer(ctx, nc, "q_x_loaded")
        row_stats = sig("row_stats", GB)
        stats_complete = sig("row_stats_complete", 1)
        row_mv = sig("row_mean_var", GB)
        row_veps = sig("row_var_eps", 1)
        row_rstd = sig("row_rstd", 1)
        xn_ready = sig("xn_ready", GB, 2 * GB)
        xn_turned = sig("xn_turned", EC, EC)
        x_high = sig("x_high_ready", EC)
        x_low = sig("x_low_ready", EC, EC)
        q_filled = sig("q_filled", MC, 2 * MC)
        q_rotated = sig("q_rotated", MC, 4)
        p_filled = sig("q_absorbed", HP, 2)
        p_copied = sig("q_copied", HP, 2)
        stored = [Signal(ctx, nc, f"q_stored{i}", 32, 16) for i in range(2)]
        block = ctx.enter_context(nc.Block())

        @block.sync
        def _(sp):
            def load(k, parity):
                sp.wait_ge(xn_ready.sem, xn_ready.at(k - 2, GB))
                src = d["x1"][bass.ds(k * GB, GB)].rearrange("b s e -> s b e")
                sp.dma_start(x[:, parity], src).then_inc(x_loaded.sems[parity], 16)

            def slot(k, parity, more):
                if more:
                    load(k + 1, 1 - parity)
                for r in range(4):
                    buf = r % 2
                    sp.wait_ge(p_copied.sem, p_copied.at(k, 2 * r + 2))
                    dst = d["qp"][bass.ds(k * GB, GB), :, 4 * r * S:4 * (r + 1) * S]
                    sp.dma_start(dst.rearrange("b e n -> e b n"), qs[:, buf].rearrange("e b h s -> e b (h s)")
                                 ).then_inc(stored[buf].sem, 16)

            for s in stored:
                sp.sem_inc(s.sem, s.credit)
            sp.dma_start(ident[:], d["ident"]).then_inc(ident_loaded.sem, 16)
            load(0, 0)
            for weights_ahead in ahead:
                weights_ahead.load(sp)
            for_groups(sp, slot)
            for buf in range(2):
                sp.wait_ge(stored[buf].sem, stored[buf].at(NG - 1, 32))

        @block.gpsimd
        def _(pool):
            pool.memset(mhalf[:], -0.5).then_inc(constants.sem, 1)
            pool.wait_ge(constants.sem, 1)

            def rows_rstd(k):
                pool.wait_ge(row_veps.sem, row_veps.at(k, 1))
                pool.tensor_tensor(rstd[:], veps[:], mhalf[:], ALU.pow).then_inc(row_rstd.sem, 1)

            def slot(k, parity, more):
                if more:
                    rows_rstd(k + 1)

            rows_rstd(0)
            for_groups(pool, slot)

        @block.scalar
        def _(act):
            act.sem_inc(p_copied.sem, p_copied.credit)

            def copy_high(k, parity):
                act.wait_ge(q_filled.sem, q_filled.at(k - 2, MC))
                for c in range(EC):
                    act.wait_ge(xn_turned.sem, xn_turned.at(k, c + 1))
                    act.copy(xh[:, parity, c], pT[:, c, 0:GT]).then_inc(x_high.sem, 1)

            def slot(k, parity, more):
                for p in range(HP):
                    buf = (p // 2) % 2
                    if p % 2 == 0:
                        act.wait_ge(stored[buf].sem, stored[buf].at(k, 16 * (p // 4)))
                    act.wait_ge(p_filled.sem, p_filled.at(k, p + 1))
                    for side in range(2):
                        cp = act.copy(qs[:, buf, :, 2 * (p % 2) + side],
                                      pp[DC * side:DC * side + DC, p % 2, 0:GT].rearrange("e (b s) -> e b s", b=GB))
                    cp.then_inc(p_copied.sem, 1)
                    if p == 4 and more:
                        copy_high(k + 1, 1 - parity)

            copy_high(0, 0)
            for_groups(act, slot)

        @block.vector
        def _(dve):
            for s in (xn_ready, x_low, q_rotated):
                dve.sem_inc(s.sem, s.credit)

            def row_statistics(k, parity):
                dve.wait_ge(x_loaded.sems[parity], x_loaded.done(k, parity))
                for b in range(GB):
                    dve.bn_stats(stats[:, b], x[:, parity, b]).then_inc(row_stats.sem, 1)
                dve.wait_ge(row_stats.sem, row_stats.at(k, GB))
                dve.sem_inc(stats_complete.sem, 1)
                for b in range(GB):
                    dve.bn_aggr(mv[:, b], stats[:, b]).then_inc(row_mv.sem, 1)
                dve.wait_ge(row_mv.sem, row_mv.at(k, GB))
                dve.tensor_scalar(veps[:], mv[:, :, 1], EPS, None, ALU.add).then_inc(row_veps.sem, 1)

            def normalise(k, parity):
                dve.wait_ge(row_rstd.sem, row_rstd.at(k, 1))
                dve.wait_ge(xn_turned.sem, xn_turned.at(k - 1, EC))
                for b in range(GB):
                    dve.tensor_scalar(xn[:, b], x[:, parity, b], mv[:, b, 0:1], rstd[:, b:b + 1],
                                      ALU.subtract, ALU.mult).then_inc(xn_ready.sem, 1)

            def split_low(k, parity):
                dve.wait_ge(q_filled.sem, q_filled.at(k - 2, MC))
                for c in range(EC):
                    dve.wait_ge(x_high.sem, x_high.at(k, c + 1))
                    dve.tensor_tensor(xl[:, parity, c], pT[:, c, 0:GT], xh[:, parity, c].bitcast(F32),
                                      ALU.subtract).then_inc(x_low.sem, 1)

            def table(t, c, rows):
                return t[rows, c].unsqueeze(1).broadcast_to([rows.stop - rows.start, GB, S])

            def rotate(k, p):
                full, top, bottom = slice(0, P), slice(0, DC), slice(DC, P)
                steps = (((full, cosq, full, 0), (full, sinq, full, 1)),
                         ((top, cosq, top, 2), (top, sinq, bottom, 2), (bottom, cosq, top, 5), (bottom, sinq, bottom, 5)),
                         ((full, cosq, full, 3), (full, sinq, full, 4)))
                dve.wait_ge(p_filled.sem, p_filled.at(k, p - 1))
                for c, ops in enumerate(steps):
                    m = 3 * p + c
                    dve.wait_ge(q_filled.sem, q_filled.at(k, m + 1))
                    for rows, tab, to, place in ops:
                        mul = dve.tensor_tensor(
                            rot[to, p % 2, place].rearrange("e (b s) -> e b s", b=GB),
                            pq[rows, m % 4, 0:GT].rearrange("e (b s) -> e b s", b=GB), table(tab, c, rows), ALU.mult)
                    mul.then_inc(q_rotated.sem, 1)

            def slot(k, parity, more):
                for p in range(HP):
                    rotate(k, p)
                    if p == 1 and more:
                        row_statistics(k + 1, 1 - parity)
                    if p == 2 and more:
                        normalise(k + 1, 1 - parity)
                    if p == 6 and more:
                        split_low(k + 1, 1 - parity)

            row_statistics(0, 0)
            normalise(0, 0)
            split_low(0, 0)
            for_groups(dve, slot)

        @block.tensor
        def _(pe):
            pe.wait_ge(ident_loaded.sem, 16)
            for s in (xn_turned, q_filled, p_filled):
                pe.sem_inc(s.sem, s.credit)

            def turn_xn(k):
                pe.wait_ge(xn_ready.sem, xn_ready.at(k, GB))
                pe.wait_ge(x_low.sem, x_low.at(k - 1, EC))
                for c in range(EC):
                    for b in range(GB):
                        mm = pe.transpose(pT[:, c, b * S:(b + 1) * S], xn[:, b, c * P:(c + 1) * P], ident[0:S, 0:S])
                    mm.then_inc(xn_turned.sem, 1)

            def project(k, parity, m):
                pe.wait_ge(q_rotated.sem, q_rotated.at(k, m - 3))
                cols = slice(m * P, (m + 1) * P)
                terms = [(w, xx, kc) for w, xx in ((wch, xh), (wch, xl), (wcl, xh)) for kc in range(EC)]
                for n, (w, xx, kc) in enumerate(terms):
                    mm = pe.matmul(pq[:, m % 4, 0:GT], w[:, kc, cols], xx[:, parity, kc],
                                   start=n == 0, stop=n == len(terms) - 1)
                mm.then_inc(q_filled.sem, 1)

            def absorb(k, p):
                pe.wait_ge(q_rotated.sem, q_rotated.at(k, 3 * p + 3))
                pe.wait_ge(p_copied.sem, p_copied.at(k, p - 1))
                for j in range(3):
                    for side in range(2):
                        mm = pe.matmul(pp[DC * side:DC * side + DC, p % 2, 0:GT], ac[:, 2 * p + side, j],
                                       rot[:, p % 2, 3 * side + j], start=j == 0, stop=j == 2)
                mm.then_inc(p_filled.sem, 1)

            def slot(k, parity, more):
                pe.wait_ge(x_low.sem, x_low.at(k, EC))
                for p in range(HP):
                    for c in range(3):
                        project(k, parity, 3 * p + c)
                    if p >= 1:
                        absorb(k, p - 1)
                    if p == 3 and more:
                        turn_xn(k + 1)
                absorb(k, HP - 1)

            turn_xn(0)
            for_groups(pe, slot)


def layout_queries(i):
    wqr = i["L0_xattn_W_qr"]
    cols = []
    for h in range(H):
        e = np.arange(P) if h % 2 == 0 else np.arange(DC, DQ)
        rest = np.arange(P, DQ) if h % 2 == 0 else np.arange(DC)
        rows = np.concatenate([e, (e + DQ // 2) % DQ, rest, (rest + DQ // 2) % DQ])
        cols.append(wqr[h][rows].T)
    wqr = np.stack(cols).reshape(2, HP, R, 3, P).transpose(0, 2, 1, 3, 4).reshape(2 * R, HP, 3, P)
    wkr = np.zeros((2, R, HP, 2, DC), np.float32)
    for side in range(2):
        wkr[side, :, :, side] = np.transpose(i["L0_xattn_W_kr"][side * HP:(side + 1) * HP], (2, 0, 1))
    sin, cos = rope_tables(S, DQ)
    e = np.arange(DQ)
    turned = (sin[:, (e + DQ // 2) % DQ] * np.where(e < DQ // 2, 1, -1)).astype(np.float32)

    def by_chunk(t):
        return np.ascontiguousarray(np.concatenate([t, t], 1).T.reshape(3, P, S).transpose(1, 0, 2)).astype(np.float32)

    return {
        "xWq": i["L0_xattn_Wq"], "w_kc_q": i["L0_xattn_w_kc_q"],
        "W_qrT": np.ascontiguousarray(wqr), "W_krT": wkr.reshape(2 * R, HP, 2 * DC),
        "cosq": by_chunk(cos), "sinq": by_chunk(turned), "ident": np.eye(P, dtype=np.float32),
    }


LC = 12
LP = -(-L // LC)
LFULL = L // LC
LREST = L - LFULL * LC
QROWS = H * S
MR = -(-QROWS // 13)
MR += MR % 2
MB = -(-QROWS // MR)
HALF = QROWS // 2
BANK = HALF // 2
PR = 4


def rows_of(c):
    return LFULL + (1 if c < LREST else 0)


def start_of(c):
    return c * LFULL + min(c, LREST)


def block_rows(r):
    return min(MR, QROWS - r * MR)


class Ring:

    def __init__(self, ctx, nc, name, units, last_units, last):
        self.index = {u: n for n, u in enumerate(units)}
        self.last_index = {u: n for n, u in enumerate(last_units)}
        self.last = last
        self.each = len(units) // 2
        assert len(units) % 2 == 0
        self.filled = [ctx.enter_context(nc.semaphore(f"{name}_filled{i}")) for i in range(2)]
        self.read = [ctx.enter_context(nc.semaphore(f"{name}_read{i}")) for i in range(2)]

    def place(self, n, unit):
        if isinstance(n, int) and n >= self.last:
            i = self.last_index[(n,) + unit]
            return i % 2, (self.last + 1) * self.each + i // 2 + 1
        i = self.index[unit]
        return i % 2, n * self.each + (self.each + i // 2 + 1)


def weights_for_cross(ctx, nc, d):
    ahead = Ahead(ctx, nc, "x")
    ahead.wkc = ahead.tensor("wkc", [K, H, DC], d["w_kc_kv"].rearrange("h k e -> k h e"))
    ahead.woT = ahead.tensor("woT", [K, H, E], d["xWoT"].rearrange("(h k) e -> k h e", k=K))
    ahead.ident = ahead.tensor("ident", [P, P], d["ident"])
    ahead.cosk = ahead.tensor("cosk", [LP, LC, DC], d["cosk"])
    ahead.sink = ahead.tensor("sink", [LP, LC, DC], d["sink"])
    return ahead


def phase_cross_attention(nc, d, ahead):
    with ExitStack() as ctx:
        def sb(name, shape, dt=F32):
            return ctx.enter_context(nc.sbuf_tensor("x_" + name, shape, dt))

        def ps(name, shape):
            return ctx.enter_context(nc.psum_tensor("x_" + name, shape, F32))

        def sig(name, each, credit=0):
            return Signal(ctx, nc, "x_" + name, each, credit)

        def transfer(name, amount, credit=0):
            return Transfer(ctx, nc, "x_" + name, credit, amount)

        ident, cosk, sink, wkc, woT = ahead.ident, ahead.cosk, ahead.sink, ahead.wkc, ahead.woT
        ones = sb("ones", [P, DC])
        wco = sb("wco", [P, H // 2, E])
        raw = sb("raw", [LP, 2, LC, DC])
        t1 = sb("t1", [LP, LC, DC])
        t2 = sb("t2", [LP, LC, DC])
        rotated = sb("rotated", [LP, LC, DC])
        kv = sb("kv", [LP, 2, LC, DC])
        ks = sb("ks", [LP, LC, 2 * DC])
        ka = sb("ka", [P, 2, L], F32R)
        kb = sb("kb", [P, 2, L], F32R)
        qraw = sb("qraw", [P, QROWS])
        qa = sb("qa", [P, 2, QROWS], F32R)
        qb = sb("qb", [P, 2, QROWS], F32R)
        mx = sb("mx", [MR, MB, 3])
        negm = sb("negm", [MR, MB])
        mrow = sb("mrow", [MB, MR], F32R)
        prob = sb("prob", [LP, PR, QROWS])
        acc = sb("acc", [LP, 2, QROWS])
        ctxs = sb("ctxs", [P, 2, BANK])
        rden = sb("rden", [P, 2, BANK])
        ctxn = sb("ctxn", [P, 2, BANK])
        xr = sb("xr", [S, 2, E])
        x2 = sb("x2", [S, 2, E])

        psc = ps("scores", [P, 2, 2, 512])
        pav = ps("context", [P, 2, 512])
        ring = ps("ring", [P, 2, 512])

        ORDER = [("scores", j) for j in range(4)] + [("context", j) for j in range(2)]
        PIECES = len(ORDER)
        C_M = 10
        side = {(c, i): [] for c in range(LC) for i in range(PIECES)}
        for place, u in (((1, 3), ("kvT", 0)), ((2, 0), ("kvT", 1)), ((2, 3), ("kvT", 2)), ((C_M, 2), ("mT",)),
                         ((C_M, 3), ("den", 0)), ((C_M, 5), ("den", 1)), ((0, 4), ("out",))):
            side[place].append(u)
        ticks = [(c, i) for c in range(3, C_M) for i in range(PIECES) for _ in range(1 + (ORDER[i][0] == "context"))]
        for m in range(3 * MB):
            side[ticks[m * len(ticks) // (3 * MB)]].append(("max", m // 3, m % 3))
        beside = {c: [u for i in range(PIECES) for u in side[c, i]] for c in range(LC)}
        units = [u for c in range(LC) for u in beside[c]]
        ends = [("out",), ("den", 0), ("den", 1)]
        rg = Ring(ctx, nc, "x_ring", units, [(n,) + u for n in (B - 1, B, B + 1) for u in ends], B - 1)

        memset = sig("memset", 0)
        raw_zeroed = sig("raw_zeroed", 0)
        rows_set = sig("constant_rows_set", 0)
        wco_filled = sig("wco_filled", 0)
        wco_copied = sig("wco_copied", 0)
        q_loaded = transfer("q_loaded", 32)
        kv_loaded = transfer("kv_loaded", 32)
        xr_loaded = transfer("xr_loaded", 16, 16)
        m_stored = transfer("m_stored", 16)
        m_loaded = transfer("m_loaded", 16)
        x2_stored = transfer("x2_stored", 16, 32)
        rope_terms = sig("rope_terms", 3, 3)
        kv_roped = sig("kv_roped", 1, 1)
        q_high = sig("q_high", 1, 1)
        q_low = sig("q_low", 1, 1)
        kv_kept = sig("kv_kept", 1, 1)
        kv_high = sig("kv_high", 1, 1)
        kv_low = sig("kv_low", 1, 1)
        max_ready = sig("maxima_ready", 1, 1)
        ctx_normed = sig("context_normed", 2, 2)
        s_filled = sig("scores_filled", 2 * LC)
        exp_done = sig("exp_done", 2 * LC, 2)
        av_done = sig("context_added", LC, 3)
        acc_done = sig("sums_added", LC - 1, 3)
        ctx_saved = sig("context_saved", 1)

        span = [(start_of(4 * i), start_of(4 * i + 3) + rows_of(4 * i + 3)) for i in range(3)]
        block = ctx.enter_context(nc.Block())
        N_MEMSET = 6

        def in_turn(eng, slot):
            slot(-1, 1, True)
            slot(0, 0, True)
            with eng.Fori(0, (B - 2) // 2) as i:
                for parity in (1, 0):
                    slot(i * 2 + (2 - parity), parity, True)
            slot(B - 1, 1, False)

        def is_at(n, value):
            return isinstance(n, int) and n == value

        @block.sync
        def _(sp):

            def load_kv(n, parity):
                wait(sp, kv_roped.sem, kv_roped.at(n - 3, 1))
                rows = d["ctx"][bass.ds(n, 1)].rearrange("b l e -> (b l) e")
                sp.dma_start(raw[0:LFULL, parity].rearrange("p c e -> p (c e)"),
                             rows[0:LFULL * LC].rearrange("(p c) e -> p (c e)", c=LC)).then_inc(kv_loaded.sems[parity], 16)
                sp.dma_start(raw[LFULL:LP, parity, 0:LREST].rearrange("p c e -> p (c e)"),
                             rows[LFULL * LC:L].rearrange("(p c) e -> p (c e)", c=LREST)
                             ).then_inc(kv_loaded.sems[parity], 16)

            def load_q(n, parity):
                wait(sp, q_low.sem, q_low.at(n - 2, 1))
                for rows in (slice(0, DC), slice(DC, P)):
                    sp.dma_start(qraw[rows], d["qp"][bass.ds(n, 1)].rearrange("b e n -> (b e) n")
                                 ).then_inc(q_loaded.sems[parity], 16)

            def load_xr(n, parity):
                bank, value = rg.place(n, ("out",))
                wait(sp, rg.read[bank], value)
                sp.dma_start(xr[:, parity], d["x1"][bass.ds(n, 1)].rearrange("b s e -> (b s) e")
                             ).then_inc(xr_loaded.sems[parity], 16)

            def store_x2(n, parity):
                bank, value = rg.place(n + 2, ("out",))
                sp.wait_ge(rg.read[bank], value)
                sp.dma_start(d["x2"][bass.ds(n, 1)].rearrange("b s e -> (b s) e"), x2[:, parity]
                             ).then_inc(x2_stored.sems[parity], 16)

            def load_m(n, parity):
                bank, value = rg.place(n - 1, ("mT",))
                sp.wait_ge(rg.read[bank], value)
                sp.dma_start(d["m"][parity], mrow[:].bitcast(F32)).then_inc(m_stored.sems[parity], 16)
                sp.wait_ge(m_stored.sems[parity], m_stored.done(n, parity))
                sp.dma_start(qb[DC:DC + 1, parity].bitcast(F32),
                             d["m"][parity].rearrange("r m -> (r m)")[0:QROWS].unsqueeze(0)
                             ).then_inc(m_loaded.sems[parity], 16)

            def slot(n, parity, store, ahead=True):
                if ahead:
                    load_kv(n + 2, parity)
                    load_q(n + 2, parity)
                load_xr(n, parity)
                if store:
                    store_x2(n - 2, parity)
                load_m(n + 1, 1 - parity)

            for parity in range(2):
                sp.sem_inc(x2_stored.sems[parity], x2_stored.credit)
                sp.sem_inc(xr_loaded.sems[parity], xr_loaded.credit)
            load_q(0, 0)
            sp.wait_ge(raw_zeroed.sem, 1)
            load_kv(0, 0)
            load_kv(1, 1)
            load_q(1, 1)
            sp.wait_ge(memset.sem, N_MEMSET)
            sp.wait_ge(rows_set.sem, 3)
            load_m(0, 0)
            slot(0, 0, False)
            slot(1, 1, False)
            with sp.Fori(1, (B - 2) // 2) as i:
                for parity in range(2):
                    slot(i * 2 + parity, parity, True)
            slot(B - 2, 0, True, False)
            load_xr(B - 1, 1)
            store_x2(B - 3, 1)
            store_x2(B - 2, 0)
            store_x2(B - 1, 1)
            for parity in range(2):
                sp.wait_ge(x2_stored.sems[parity], x2_stored.done(B - 2 + parity, parity))

        @block.gpsimd
        def _(pool):
            pool.memset(raw[:], 0.0).then_inc(raw_zeroed.sem, 1)
            for t, v in ((ones[:], 1.0), (ctxn[:], 0.0), (acc[:], 1.0), (ctxs[:], 0.0), (xr[:], 0.0), (mx[:], 0.0)):
                pool.memset(t, v).then_inc(memset.sem, 1)
            pool.sem_inc(acc_done.sem, acc_done.credit)
            pool.wait_ge(raw_zeroed.sem, 1)
            pool.wait_ge(memset.sem, N_MEMSET)
            for t in (kb, qb):
                pool.memset(t[DC:P].bitcast(F32), 0.0).then_inc(rows_set.sem, 1)
            pool.wait_ge(rows_set.sem, 2)
            pool.memset(kb[DC:DC + 1].bitcast(F32), 1.0).then_inc(rows_set.sem, 1)

            def slot(n, parity, more):
                if is_at(n, -1):
                    return
                bank, value = rg.place(n - 1, ("den", 1))
                pool.wait_ge(rg.filled[bank], value)
                for c in range(1, LC):
                    rows = rows_of(c)
                    pool.wait_ge(exp_done.sem, exp_done.at(n, 2 * c + 2))
                    first = prob[0:rows, 0] if c == 1 else acc[0:rows, parity]
                    if c > 1:
                        pool.wait_ge(acc_done.sem, acc_done.at(n, c - 1))
                    pool.tensor_tensor(acc[0:rows, parity], first, prob[0:rows, c % PR],
                                       ALU.add).then_inc(acc_done.sem, 1)

            in_turn(pool, slot)

        @block.scalar
        def _(act):
            act.sem_inc(exp_done.sem, exp_done.credit)

            def exponentials(n, c, u):
                rows = rows_of(c)
                if u == 0:
                    act.wait_ge(av_done.sem, av_done.at(n, c - 3))
                    act.wait_ge(acc_done.sem, acc_done.at(n, max(c - 4, 1) if c >= PR else c - 3))
                act.wait_ge(s_filled.sem, s_filled.at(n, 2 * c + u + 1))
                act.activation(prob[0:rows, c % PR, u * HALF:(u + 1) * HALF].rearrange("p (j s) -> p j s", j=2),
                               psc[0:rows, u, :, 0:BANK], ACT.Exp).then_inc(exp_done.sem, 1)

            def copy_turned(n, parity, i):
                if i == 0:
                    wait(act, s_filled.sem, s_filled.at(n, 0))
                bank, value = rg.place(n, ("kvT", i))
                act.wait_ge(rg.filled[bank], value)
                a, b = span[i]
                act.copy(ka[:, parity, a:b], ring[:, bank, 0:b - a])
                act.copy(kb[0:DC, parity, a:b], ring[0:DC, bank, 0:b - a]).then_inc(rg.read[bank], 1)

            def save_context(n):
                act.wait_ge(av_done.sem, av_done.at(n, 0))
                act.wait_ge(ctx_normed.sem, ctx_normed.at(n - 1, 2))
                act.copy(ctxs[:], pav[:, :, 0:BANK]).then_inc(ctx_saved.sem, 1)

            def slot(n, parity, more):
                for c in range(LC):
                    if c == 1 and not is_at(n, -1) and not is_at(n, 0):
                        save_context(n)
                    for u in range(2):
                        if not is_at(n, -1):
                            exponentials(n, c, u)
                        if 2 * c + u in (3, 4, 5) and more:
                            copy_turned(n, 1 - parity, 2 * c + u - 3)
                    if c == 0 and more:
                        act.wait_ge(kv_roped.sem, kv_roped.at(n, 1))
                        bank, value = rg.place(n - 1, ("kvT", 2))
                        wait(act, rg.filled[bank], value)
                        act.copy(ks[:, :, 0:DC].bitcast(F32R), rotated[:]).then_inc(kv_high.sem, 1)
                    if c == 1 and more:
                        wait(act, av_done.sem, av_done.at(n, 0))
                        act.copy(kv[:, 1 - parity], rotated[:]).then_inc(kv_kept.sem, 1)

            in_turn(act, slot)
            save_context(B)

        @block.vector
        def _(dve):
            ahead.wait(dve)

            def rope(n, parity):
                dve.wait_ge(kv_loaded.sems[parity], kv_loaded.done(n + 1, parity))
                half = DC // 2
                dve.tensor_tensor(t1[:], raw[:, parity], cosk[:], ALU.mult).then_inc(rope_terms.sem, 1)
                for to, frm in ((slice(0, half), slice(half, DC)), (slice(half, DC), slice(0, half))):
                    dve.tensor_tensor(t2[:, :, to], raw[:, parity, :, frm], sink[:, :, to],
                                      ALU.mult).then_inc(rope_terms.sem, 1)
                wait(dve, kv_kept.sem, kv_kept.at(n - 1, 1))
                dve.wait_ge(rope_terms.sem, rope_terms.at(n, 3))
                dve.tensor_tensor(rotated[:], t1[:], t2[:], ALU.add).then_inc(kv_roped.sem, 1)
                dve.wait_ge(kv_high.sem, kv_high.at(n, 1))
                dve.tensor_tensor(ks[:, :, DC:2 * DC].bitcast(F32R), rotated[:], ks[:, :, 0:DC],
                                  ALU.subtract).then_inc(kv_low.sem, 1)

            def split_q(n, parity):
                dve.wait_ge(q_loaded.sems[parity], q_loaded.done(n + 1, parity))
                wait(dve, s_filled.sem, s_filled.at(n, 0))
                dve.tensor_copy(qa[:, parity], qraw[:]).then_inc(q_high.sem, 1)
                dve.wait_ge(q_high.sem, q_high.at(n, 1))
                dve.tensor_tensor(qb[0:DC, parity], qraw[0:DC], qa[0:DC, parity].bitcast(F32),
                                  ALU.subtract).then_inc(q_low.sem, 1)

            def normalise(n, j):
                bank, value = rg.place(n, ("den", j))
                dve.wait_ge(rg.filled[bank], value)
                if j == 0:
                    wait(dve, ctx_saved.sem, ctx_saved.at(n, 0))
                dve.reciprocal(rden[:, j], ring[:, bank, 0:BANK]).then_inc(rg.read[bank], 1)
                dve.wait_ge(rg.read[bank], value)
                before, value = rg.place(n, ("out",))
                dve.wait_ge(rg.filled[before], value)
                dve.tensor_tensor(ctxn[:, j], ctxs[:, j], rden[:, j], ALU.mult).then_inc(ctx_normed.sem, 1)

            def output(n, parity):
                bank, value = rg.place(n, ("out",))
                dve.wait_ge(rg.filled[bank], value)
                wait(dve, xr_loaded.sems[parity], xr_loaded.done(n - 2, parity))
                wait(dve, x2_stored.sems[parity], x2_stored.done(n - 4, parity))
                dve.tensor_tensor(x2[:, parity], ring[0:S, bank, 0:E], xr[:, parity],
                                  ALU.add).then_inc(rg.read[bank], 1)

            def maximum(n, r, i):
                bank, value = rg.place(n, ("max", r, i))
                dve.wait_ge(rg.filled[bank], value)
                a, b = span[i]
                dve.tensor_reduce(mx[0:block_rows(r), r, i:i + 1], ring[0:block_rows(r), bank, 0:b - a], AX.X,
                                  ALU.max).then_inc(rg.read[bank], 1)

            def slot(n, parity, more):
                for c in range(LC):
                    if c == 0 and more:
                        rope(n, 1 - parity)
                        split_q(n, 1 - parity)
                    for u in beside[c]:
                        if u[0] == "den":
                            normalise(n, u[1])
                        elif u[0] == "out":
                            output(n, parity)
                        elif u[0] == "max" and more:
                            maximum(n, u[1], u[2])
                        elif u[0] == "mT" and more:
                            bank, value = rg.place(n, u)
                            dve.wait_ge(rg.filled[bank], value)
                            dve.tensor_copy(mrow[:], ring[0:MB, bank, 0:MR]).then_inc(rg.read[bank], 1)
                    if c == C_M - 1 and more:
                        for i in (1, 2):
                            bank, value = rg.place(n, ("max", MB - 1, i))
                            dve.wait_ge(rg.read[bank], value)
                        dve.tensor_reduce(negm[:], mx[:], AX.X, ALU.max, negate=True).then_inc(max_ready.sem, 1)

            for h in range(H // 2):
                dve.wait_ge(wco_filled.sem, h + 1)
                dve.tensor_copy(wco[:, h], ring[:, h % 2, 0:E]).then_inc(wco_copied.sem, 1)
            dve.wait_ge(memset.sem, N_MEMSET)
            in_turn(dve, slot)
            output(B, 0)
            for j in range(2):
                normalise(B, j)
            output(B + 1, 1)

        @block.tensor
        def _(pe):
            ahead.wait(pe)
            pe.sem_inc(av_done.sem, av_done.credit)
            for h in range(H // 2):
                wait(pe, wco_copied.sem, h - 1)
                for s in range(2):
                    mm = pe.matmul(ring[DC * s:DC * s + DC, h % 2, 0:E], wkc[:, h + s * (H // 2)],
                                   woT[:, h + s * (H // 2)], start=True, stop=True)
                mm.then_inc(wco_filled.sem, 1)
            pe.wait_ge(wco_copied.sem, H // 2)
            pe.wait_ge(memset.sem, N_MEMSET)

            def scores(n, parity, c, u, j):
                rows, a = rows_of(c), start_of(c)
                cols = slice(u * HALF + j * BANK, u * HALF + (j + 1) * BANK)
                out = psc[0:rows, u, j, 0:BANK]
                if j == 0:
                    pe.wait_ge(exp_done.sem, exp_done.at(n, 2 * c + u - 1))
                pe.matmul(out, ka[:, parity, a:a + rows], qa[:, parity, cols], start=True, stop=False)
                if c == 0 and u == 0 and j == 0:
                    pe.wait_ge(m_loaded.sems[parity], m_loaded.done(n, parity))
                mm = pe.matmul(out, kb[:, parity, a:a + rows], qb[:, parity, cols], start=False, stop=True)
                if j == 1:
                    mm.then_inc(s_filled.sem, 1)

            def context(n, parity, c, j):
                rows = rows_of(c)
                if j == 0:
                    pe.wait_ge(exp_done.sem, exp_done.at(n, 2 * c + 2))
                if c == 0 and j == 0:
                    wait(pe, ctx_saved.sem, ctx_saved.at(n, 0))
                for s in range(2):
                    cols = slice(s * HALF + j * BANK, s * HALF + (j + 1) * BANK)
                    mm = pe.matmul(pav[DC * s:DC * s + DC, j, 0:BANK], kv[0:rows, parity, c],
                                   prob[0:rows, c % PR, cols], start=c == 0, stop=c == LC - 1)
                if j == 1:
                    mm.then_inc(av_done.sem, 1)

            def piece(n, parity, c, i):
                kind, which = ORDER[i]
                if kind == "scores":
                    scores(n, parity, c, which // 2, which % 2)
                elif c >= 1:
                    context(n, parity, c - 1, which)
                elif not is_at(n, 0):
                    context(n - 1, 1 - parity, LC - 1, which)

            def make(n, parity, u):
                bank, value = rg.place(n, u)
                wait(pe, rg.read[bank], value - 1)
                if u[0] == "kvT":
                    pe.wait_ge(kv_low.sem, kv_low.at(n, 1))
                    a = span[u[1]][0]
                    for c in range(4 * u[1], 4 * u[1] + 4):
                        rows, b = rows_of(c), start_of(c) - a
                        mm = pe.transpose(ring[:, bank, b:b + rows], ks[0:rows, c], ident[0:rows, 0:rows])
                elif u[0] == "den":
                    wait(pe, acc_done.sem, acc_done.at(n, 0))
                    for s in range(2):
                        cols = slice(s * HALF + u[1] * BANK, s * HALF + (u[1] + 1) * BANK)
                        mm = pe.matmul(ring[DC * s:DC * s + DC, bank, 0:BANK], ones[0:LP], acc[:, 1 - parity, cols],
                                       start=True, stop=True)
                elif u[0] == "out":
                    for h in range(H // 2):
                        if h % 4 == 0:
                            wait(pe, ctx_normed.sem, ctx_normed.at(n - 1, h // 4 + 1))
                        mm = pe.matmul(ring[0:S, bank, 0:E], ctxn[:, h // 4, (h % 4) * S:(h % 4 + 1) * S],
                                       wco[:, h], start=h == 0, stop=h == H // 2 - 1)
                elif u[0] == "max":
                    if u[1] == 0 and u[2] == 0:
                        pe.wait_ge(q_low.sem, q_low.at(n, 1))
                    a, b = span[u[2]]
                    r = u[1]
                    mm = pe.matmul(ring[0:block_rows(r), bank, 0:b - a],
                                   qa[:, 1 - parity, r * MR:r * MR + block_rows(r)], ka[:, 1 - parity, a:b],
                                   start=True, stop=True)
                else:
                    pe.wait_ge(max_ready.sem, max_ready.at(n, 1))
                    mm = pe.transpose(ring[0:MB, bank, 0:MR], negm[:], ident[0:MR, 0:MR])
                mm.then_inc(rg.filled[bank], 1)

            def slot(n, parity, more):
                if is_at(n, 0):
                    pe.wait_ge(rows_set.sem, 3)
                for c in range(LC):
                    for i in range(PIECES):
                        if not is_at(n, -1):
                            piece(n, parity, c, i)
                        for u in side[c, i]:
                            if more or u[0] in ("den", "out"):
                                make(n, parity, u)

            in_turn(pe, slot)
            for j in range(2):
                context(B - 1, 1, LC - 1, j)
            for u in ends:
                make(B, 0, u)
            make(B + 1, 1, ("out",))


def layout_cross(i):
    sin, cos = rope_tables(L, DC)
    half = DC // 2
    sin = np.concatenate([-sin[:, :half], sin[:, half:]], 1)

    def by_row(t):
        padded = np.concatenate([t, np.zeros((LP * LC - L, DC), np.float32)])
        out = padded[:LFULL * LC].reshape(LFULL, LC, DC)
        last = np.zeros((1, LC, DC), np.float32)
        last[0, :LREST] = t[LFULL * LC:]
        return np.ascontiguousarray(np.concatenate([out, last])).astype(np.float32)

    return {"ctx": i["ctx_512"], "cosk": by_row(cos), "sink": by_row(sin), "w_kc_kv": i["L0_xattn_w_kc_kv"],
            "xWoT": np.ascontiguousarray(i["L0_xattn_Wo"].T), "ident": np.eye(P, dtype=np.float32)}


FC = 6
FM = -(-F // FC)
FW_EPS = 1e-8


def hidden_rows(m):
    return min(FM, F - m * FM)


def weights_for_ffn(ctx, nc, d):
    ahead = Ahead(ctx, nc, "f")
    ahead.ident = ahead.tensor("ident", [P, P], d["ident"])
    ahead.w1 = ahead.tensor("w1", [P, EC, F], d["w1T"].rearrange("(c p) f -> p c f", p=P))
    ahead.w2 = ahead.tensor("w2", [P, EC, F], d["w2T"].rearrange("(c p) f -> p c f", p=P))
    return ahead


def phase_ffn(nc, d, ahead):
    with ExitStack() as ctx:
        def sb(name, shape, dt=F32):
            return ctx.enter_context(nc.sbuf_tensor("f_" + name, shape, dt))

        def ps(name, shape):
            return ctx.enter_context(nc.psum_tensor("f_" + name, shape, F32))

        def sig(name, each, credit=0):
            return Signal(ctx, nc, "f_" + name, each, credit)

        ident = ahead.ident
        ones = sb("ones", [P, P])
        mhalf = sb("mhalf", [S, GB])
        w = [ahead.w1, ahead.w2, sb("w3", [P, FC, E])]
        below = sb("below", [P, 2, FC * E])
        t12 = sb("t12", [P, 2, EC, F], F32R)
        t3 = sb("t3", [P, FC, E], F32R)
        part = sb("part", [P, 3, 24])
        total = sb("total", [P, 3])
        mean = sb("mean", [P, 3])
        thr = sb("thr", [P, 3])
        nthr = sb("nthr", [P, 3])
        x = sb("x", [S, 2, GB, E])
        stats = sb("stats", [S, GB, 6])
        mv = sb("mv", [S, GB, 2])
        veps = sb("veps", [S, GB])
        rstd = sb("rstd", [S, GB])
        xn = sb("xn", [S, GB, E])
        xh = sb("xh", [P, 2, EC, GT], F32R)
        xl = sb("xl", [P, 2, EC, GT], F32R)
        th = sb("th", [FM, 2, GT])
        hid = sb("hid", [FM, 2, GT])
        hh = sb("hh", [FM, 2, FC, GT], F32R)
        hl = sb("hl", [FM, 2, FC, GT], F32R)
        y = sb("y", [S, 2, GB, E])

        pT = ps("pT", [P, EC, 512])
        ph = ps("ph", [P, 2, 2, 512])
        po = ps("po", [P, 2, 512])

        loaded = sig("weights_loaded", 0)
        constants = sig("constants_set", 0)
        w3_zeroed = sig("w3_zeroed", 0)
        quant = sig("quantising_steps", 0)
        totals = sig("totals_filled", 0)
        quantised = sig("weights_quantised", 0)
        x_loaded = Transfer(ctx, nc, "f_x_loaded")
        y_stored = Transfer(ctx, nc, "f_y_stored", 16)
        row_stats = sig("row_stats", GB)
        stats_complete = sig("row_stats_complete", 1)
        row_mv = sig("row_mean_var", GB)
        row_veps = sig("row_var_eps", 1)
        row_rstd = sig("row_rstd", 1)
        xn_ready = sig("xn_ready", GB)
        xn_turned = sig("xn_turned", EC, EC)
        x_high = sig("x_high_ready", EC)
        x_low = sig("x_low_ready", EC, EC)
        h_filled = sig("hidden_filled", FC, 2 * FC)
        gate_tanh = sig("gate_tanh", FC)
        gated = sig("hidden_gated", FC, 2)
        h_high = sig("hidden_high_ready", FC, 2)
        h_low = sig("hidden_low_ready", FC, 2)
        o_filled = sig("output_filled", GB, GB + 1)
        y_ready = sig("output_ready", GB, 2 * GB)
        x_kept = sig("x_kept", 1, 2)
        block = ctx.enter_context(nc.Block())
        LOADS = 2

        @block.sync
        def _(sp):
            def load(k, parity):
                sp.wait_ge(x_kept.sem, x_kept.at(k - 2, 1))
                src = d["x2"][bass.ds(k * GB, GB)].rearrange("b s e -> s b e")
                sp.dma_start(x[:, parity], src).then_inc(x_loaded.sems[parity], 16)

            def store(k, parity):
                sp.wait_ge(y_ready.sem, y_ready.at(k, GB))
                dst = d["out"][bass.ds(k * GB, GB)].rearrange("b s e -> s b e")
                sp.dma_start(dst, y[:, parity]).then_inc(y_stored.sems[parity], 16)

            def slot(k, parity, more):
                if more:
                    load(k + 2, parity)
                if not is_first(k):
                    store(k - 1, 1 - parity)

            whole = F // FM
            for parity in range(2):
                sp.sem_inc(y_stored.sems[parity], y_stored.credit)
            load(0, 0)
            sp.wait_ge(w3_zeroed.sem, 1)
            for dst, src in ((w[2][0:FM, 0:whole], d["w3T"][0:whole * FM].rearrange("(c p) e -> p c e", p=FM)),
                             (w[2][0:F - whole * FM, whole], d["w3T"][whole * FM:F])):
                sp.dma_start(dst, src).then_inc(loaded.sem, 16)
            load(1, 1)
            for_groups_ahead(sp, slot)
            store(NG - 1, 1)
            for parity in range(2):
                sp.wait_ge(y_stored.sems[parity], y_stored.done(NG - 2 + parity, parity))

        @block.gpsimd
        def _(pool):
            pool.sem_inc(x_kept.sem, x_kept.credit)
            pool.memset(w[2][:], 0.0).then_inc(w3_zeroed.sem, 1)
            pool.memset(mhalf[:], -0.5).then_inc(constants.sem, 1)
            pool.memset(ones[:], 1.0).then_inc(constants.sem, 1)
            pool.wait_ge(constants.sem, 2)

            def rows_rstd(k):
                pool.wait_ge(row_veps.sem, row_veps.at(k, 1))
                pool.tensor_tensor(rstd[:], veps[:], mhalf[:], ALU.pow).then_inc(row_rstd.sem, 1)

            def slot(k, parity, more):
                if more:
                    rows_rstd(k + 1)
                pool.wait_ge(xn_ready.sem, xn_ready.at(k, GB))
                pool.wait_ge(x_loaded.sems[parity], x_loaded.done(k, parity))
                pool.wait_ge(y_stored.sems[parity], y_stored.done(k - 2, parity))
                pool.tensor_tensor(y[:, parity], x[:, parity], ones[0:S, 0:1].unsqueeze(2).broadcast_to([S, GB, E]),
                                   ALU.mult).then_inc(x_kept.sem, 1)

            rows_rstd(0)
            for_groups(pool, slot)

        @block.scalar
        def _(act):
            act.sem_inc(h_high.sem, h_high.credit)

            def copy_high(k, parity):
                act.wait_ge(h_filled.sem, h_filled.at(k - 2, FC))
                for c in range(EC):
                    act.wait_ge(xn_turned.sem, xn_turned.at(k, c + 1))
                    act.copy(xh[:, parity, c], pT[:, c, 0:GT]).then_inc(x_high.sem, 1)

            def slot(k, parity, more):
                for m in range(FC):
                    n = hidden_rows(m)
                    act.wait_ge(h_filled.sem, h_filled.at(k, m + 1))
                    act.wait_ge(gated.sem, gated.at(k, m - 1))
                    act.activation(th[0:n, m % 2], ph[0:n, m % 2, 0, 0:GT], ACT.Tanh,
                                   scale=0.5).then_inc(gate_tanh.sem, 1)
                    if m == 0:
                        act.wait_ge(o_filled.sem, o_filled.at(k - 1, 0))
                    act.wait_ge(gated.sem, gated.at(k, m + 1))
                    act.copy(hh[0:n, parity, m], hid[0:n, m % 2]).then_inc(h_high.sem, 1)
                    if m == 3 and more:
                        copy_high(k + 1, 1 - parity)

            copy_high(0, 0)
            for_groups(act, slot)

        @block.vector
        def _(dve):
            for s in (x_low, gated, h_low, y_ready):
                dve.sem_inc(s.sem, s.credit)

            def row_statistics(k, parity):
                dve.wait_ge(x_loaded.sems[parity], x_loaded.done(k, parity))
                for b in range(GB):
                    dve.bn_stats(stats[:, b], x[:, parity, b]).then_inc(row_stats.sem, 1)
                dve.wait_ge(row_stats.sem, row_stats.at(k, GB))
                dve.sem_inc(stats_complete.sem, 1)
                for b in range(GB):
                    dve.bn_aggr(mv[:, b], stats[:, b]).then_inc(row_mv.sem, 1)
                dve.wait_ge(row_mv.sem, row_mv.at(k, GB))
                dve.tensor_scalar(veps[:], mv[:, :, 1], EPS, None, ALU.add).then_inc(row_veps.sem, 1)

            def normalise(k, parity):
                dve.wait_ge(row_rstd.sem, row_rstd.at(k, 1))
                dve.wait_ge(xn_turned.sem, xn_turned.at(k - 1, EC))
                for b in range(GB):
                    dve.tensor_scalar(xn[:, b], x[:, parity, b], mv[:, b, 0:1], rstd[:, b:b + 1],
                                      ALU.subtract, ALU.mult).then_inc(xn_ready.sem, 1)

            def split_low(k, parity):
                for c in range(EC):
                    dve.wait_ge(x_high.sem, x_high.at(k, c + 1))
                    dve.tensor_tensor(xl[:, parity, c], pT[:, c, 0:GT], xh[:, parity, c].bitcast(F32),
                                      ALU.subtract).then_inc(x_low.sem, 1)

            def gate(k, m):
                n = hidden_rows(m)
                dve.wait_ge(gate_tanh.sem, gate_tanh.at(k, m + 1))
                dve.wait_ge(h_low.sem, h_low.at(k, m - 1))
                dve.scalar_tensor_tensor(hid[0:n, m % 2], th[0:n, m % 2], 1.0, ph[0:n, m % 2, 1, 0:GT],
                                         ALU.add, ALU.mult).then_inc(gated.sem, 1)

            def low(k, parity, m):
                n = hidden_rows(m)
                dve.wait_ge(h_high.sem, h_high.at(k, m + 1))
                dve.tensor_tensor(hl[0:n, parity, m], hid[0:n, m % 2], hh[0:n, parity, m].bitcast(F32),
                                  ALU.subtract).then_inc(h_low.sem, 1)

            def add_output(k, parity, b):
                if b == 0:
                    dve.wait_ge(x_kept.sem, x_kept.at(k, 1))
                dve.wait_ge(o_filled.sem, o_filled.at(k, b + 1))
                dve.scalar_tensor_tensor(y[:, parity, b], po[0:S, b % 2, 0:E], 0.5, y[:, parity, b], ALU.mult,
                                         ALU.add).then_inc(y_ready.sem, 1)

            def slot(k, parity, more):
                for m in range(FC):
                    gate(k, m)
                    if m >= 1:
                        low(k, parity, m - 1)
                    if m == 0 and more:
                        row_statistics(k + 1, 1 - parity)
                    if m == 2 and more:
                        normalise(k + 1, 1 - parity)
                    if m >= 2 and not is_first(k):
                        add_output(k - 1, 1 - parity, m - 2)
                    if m == 4 and more:
                        split_low(k + 1, 1 - parity)
                low(k, parity, FC - 1)

            ahead.wait(dve)
            sizes = [EC * F, EC * F, FC * E]
            flat = [t[:].rearrange("p c n -> p (c n)") for t in w]
            steps = [0]

            def step(ins):
                steps[0] += 1
                ins.then_inc(quant.sem, 1)

            for i in range(3):
                piece = 64
                if i == 2:
                    row_statistics(0, 0)
                    normalise(0, 0)
                    dve.wait_ge(loaded.sem, 16 * LOADS)
                step(dve.tensor_reduce(part[:, i, 0:sizes[i] // piece], flat[i].rearrange("p (a n) -> p a n", n=piece),
                                       AX.X, ALU.add, apply_absolute_value=True))
            dve.wait_ge(quant.sem, steps[0])
            for i in range(3):
                step(dve.tensor_reduce(total[:, i:i + 1], part[:, i, 0:sizes[i] // 64], AX.X, ALU.add))
            split_low(0, 0)
            dve.wait_ge(totals.sem, 1)
            step(dve.tensor_scalar(mean[:], po[:, 0, 0:3], 1.0 / (F * E), FW_EPS, ALU.mult, ALU.add))
            dve.wait_ge(quant.sem, steps[0])
            step(dve.tensor_scalar(thr[:], mean[:], 0.5, None, ALU.mult))
            step(dve.tensor_scalar(nthr[:], mean[:], -0.5, None, ALU.mult))
            dve.wait_ge(quant.sem, steps[0])
            for i in range(3):
                out = (t12[:, i] if i < 2 else t3[:]).rearrange("p c n -> p (c n)")
                step(dve.tensor_scalar(below[:, i % 2, 0:sizes[i]], flat[i], nthr[:, i:i + 1], None, ALU.is_lt))
                dve.wait_ge(quant.sem, steps[0])
                dve.scalar_tensor_tensor(out, flat[i], thr[:, i:i + 1], below[:, i % 2, 0:sizes[i]], ALU.is_gt,
                                         ALU.subtract).then_inc(quantised.sem, 1)
            for_groups(dve, slot)
            for b in range(GB):
                add_output(NG - 1, 1, b)

        @block.tensor
        def _(pe):
            for s in (xn_turned, h_filled, o_filled):
                pe.sem_inc(s.sem, s.credit)

            def turn_xn(k):
                pe.wait_ge(xn_ready.sem, xn_ready.at(k, GB))
                pe.wait_ge(x_low.sem, x_low.at(k - 1, EC))
                for c in range(EC):
                    for b in range(GB):
                        mm = pe.transpose(pT[:, c, b * S:(b + 1) * S], xn[:, b, c * P:(c + 1) * P], ident[0:S, 0:S])
                    mm.then_inc(xn_turned.sem, 1)

            def hidden(k, parity, m):
                n = hidden_rows(m)
                pe.wait_ge(gated.sem, gated.at(k, m - 1))
                for i in range(2):
                    terms = [(xx, kc) for xx in (xh, xl) for kc in range(EC)]
                    for j, (xx, kc) in enumerate(terms):
                        mm = pe.matmul(ph[0:n, m % 2, i, 0:GT], t12[:, i, kc, m * FM:m * FM + n], xx[:, parity, kc],
                                       start=j == 0, stop=j == len(terms) - 1)
                mm.then_inc(h_filled.sem, 1)

            def output(k, parity, b):
                if b == 0:
                    pe.wait_ge(quantised.sem, 3)
                    pe.wait_ge(h_low.sem, h_low.at(k, FC))
                pe.wait_ge(y_ready.sem, y_ready.at(k, b - 1))
                for m in range(FC):
                    n = hidden_rows(m)
                    for hx in (hh, hl):
                        mm = pe.matmul(po[0:S, b % 2, 0:E], hx[0:n, parity, m, b * S:(b + 1) * S], t3[0:n, m],
                                       start=m == 0 and hx is hh, stop=m == FC - 1 and hx is hl)
                mm.then_inc(o_filled.sem, 1)

            ahead.wait(pe)
            turn_xn(0)

            def slot(k, parity, more):
                pe.wait_ge(x_low.sem, x_low.at(k, EC))
                for m in range(FC):
                    hidden(k, parity, m)
                    if m == 3 and more:
                        turn_xn(k + 1)
                    if 1 <= m <= GB and not is_first(k):
                        output(k - 1, 1 - parity, m - 1)

            pe.wait_ge(constants.sem, 2)
            pe.wait_ge(quant.sem, 6)
            pe.matmul(po[:, 0, 0:3], ones[:], total[:], start=True, stop=True).then_inc(totals.sem, 1)
            pe.wait_ge(quantised.sem, 2)
            for_groups(pe, slot)
            for b in range(GB):
                output(NG - 1, 1, b)


def layout_ffn(i):
    return {"w1T": np.ascontiguousarray(i["L0_ffn_w1"].T), "w2T": np.ascontiguousarray(i["L0_ffn_w2"].T),
            "w3T": np.ascontiguousarray(i["L0_ffn_w3"].T), "ident": np.eye(P, dtype=np.float32)}


def build(nc, d):
    for name, shape in (("x1", (B, S, E)), ("x2", (B, S, E)), ("qp", (B, DC, QROWS)), ("m", (2, MB, MR))):
        d[name] = nc.dram_tensor("scratch_" + name, shape, F32, kind="Internal").ap()
    with ExitStack() as whole:
        for_ffn = weights_for_ffn(whole, nc, d)
        products = whole.enter_context(ExitStack())
        with ExitStack() as ctx:
            for_queries = weights_for_queries(ctx, nc, d)
            phase_retention(nc, d, [for_queries, for_ffn])
            made = query_weights(products, nc)
            phase_query_weights(nc, d, for_queries, made)
        for_cross = weights_for_cross(whole, nc, d)
        phase_queries(nc, d, made, [for_cross])
        products.close()
        phase_cross_attention(nc, d, for_cross)
        phase_ffn(nc, d, for_ffn)


def kernel(**inputs):
    import concourse.bacc as bacc
    from concourse.bass_utils import run_bass_kernel_spmd

    i = {name: np.asarray(a) for name, a in inputs.items()}
    arrays = {}
    for layout in (layout_retention, layout_queries, layout_cross, layout_ffn):
        arrays.update(layout(i))
    nc = bacc.Bacc("TRN2", target_bir_lowering=False, num_devices=1)
    d, given = {}, {}
    for name, a in arrays.items():
        a = np.ascontiguousarray(a)
        given["in_" + name] = a
        d[name] = nc.dram_tensor("in_" + name, a.shape, mybir.dt.from_np(a.dtype), kind="ExternalInput").ap()
    d["out"] = nc.dram_tensor("out_0", (B, S, E), F32, kind="ExternalOutput").ap()
    build(nc, d)
    result = run_bass_kernel_spmd(nc, [given], core_ids=[0])
    return result.results[0]["out_0"]
```
